# Optimizing a Trainium2 kernel written in Bass

```python
import numpy as np
import jax
import jax.numpy as jnp

def _softmax(x, axis=-1):
    return jax.nn.softmax(x, axis=axis)

def _gelu(x):
    return jax.nn.gelu(x, approximate=True)

def _silu(x):
    return jax.nn.silu(x)

def _sigmoid(x):
    return jax.nn.sigmoid(x)

def _layernorm(x, axis=-1, eps=1e-05):
    m = jnp.mean(x, axis=axis, keepdims=True)
    v = jnp.var(x, axis=axis, keepdims=True)
    return (x - m) / jnp.sqrt(v + eps)

def _scatter_add(tgt, idx, src, axis=0):
    return tgt.at[idx].add(src)

def _segment_sum(src, seg, n):
    return jax.ops.segment_sum(src, seg, n)
kernel_name = 'mk_seq_preln_d1_jaxref_r2_c3e78d'

def setup_inputs(seed: int=0):
    np.random.seed(seed)
    _w = jnp.asarray

    def _L0_attn_setup():
        import jax, jax.numpy as jnp
        import numpy as np
        DIM, H, C = (512, 16, 64)
        D = DIM // H
        GATE_HID = 16
        key = jax.random.key(seed)
        ks = jax.random.split(key, 8)
        B, L = (2, 1024)

        def xav(k, fan_in, fan_out):
            return jax.random.normal(k, (fan_in, fan_out), jnp.float32) * np.sqrt(2.0 / (fan_in + fan_out))
        return {'x': jax.random.normal(ks[0], (B, L, DIM), jnp.float32), 'Wq': xav(ks[1], DIM, DIM), 'bq': jnp.zeros((DIM,), jnp.float32), 'Wk': xav(ks[2], DIM, DIM), 'bk': jnp.zeros((DIM,), jnp.float32), 'Wv': xav(ks[3], DIM, DIM), 'bv': jnp.zeros((DIM,), jnp.float32), 'Wg1': xav(ks[4], DIM, GATE_HID), 'bg1': jnp.zeros((GATE_HID,), jnp.float32), 'Wg2': xav(ks[5], GATE_HID, H * D), 'bg2': jnp.zeros((H * D,), jnp.float32)}
    _L0_attn_in = _L0_attn_setup()

    def _L0_ffn_setup():
        import jax, jax.numpy as jnp
        import numpy as np
        B, S, D = (1, 1024, 512)
        E, K, F = (64, 8, 384)
        SF = 384
        C = 256
        ROUTED_SCALE = 1.0

        def _moe_forward(x, router_w, w_gate, w_up, w_down, ws_gate_up, ws_down):
            T = x.shape[0]
            logits = x.astype(jnp.float32) @ router_w.T
            probs = jax.nn.softmax(logits, axis=-1)
            topk_w, topk_ids = jax.lax.top_k(probs, K)
            topk_w = topk_w / jnp.sum(topk_w, axis=-1, keepdims=True)
            topk_w = topk_w.astype(x.dtype)
            N = T * K
            flat_e = topk_ids.reshape(-1)
            flat_w = topk_w.reshape(-1)
            tok = jnp.arange(N) // K
            onehot = flat_e[:, None] == jnp.arange(E)[None, :]
            pos = jnp.cumsum(onehot, axis=0)[jnp.arange(N), flat_e] - 1
            valid = pos < C
            idx = jnp.where(valid, flat_e * C + pos, E * C)
            x_buf = jnp.zeros((E * C + 1, x.shape[1]), x.dtype).at[idx].set(x[tok])
            xb = x_buf[:E * C].reshape(E, C, -1)
            g = jnp.einsum('ecd,edf->ecf', xb, w_gate)
            u = jnp.einsum('ecd,edf->ecf', xb, w_up)
            h = jax.nn.silu(g) * u
            y = jnp.einsum('ecf,efd->ecd', h, w_down).reshape(E * C, -1)
            safe = jnp.where(valid, idx, 0)
            contrib = y[safe] * (flat_w * valid.astype(flat_w.dtype))[:, None]
            routed = jax.ops.segment_sum(contrib, tok, num_segments=T)
            routed = routed * ROUTED_SCALE
            gu = x @ ws_gate_up
            sg, su = (gu[:, :SF], gu[:, SF:])
            shared = jax.nn.silu(sg) * su @ ws_down
            return routed + shared
        key = jax.random.key(seed)
        ks = jax.random.split(key, 7)
        w = 0.02
        return {'hidden_states': jax.random.normal(ks[0], (B, S, D), jnp.float32), 'router_w': jax.random.normal(ks[1], (E, D), jnp.float32) * w, 'w_gate': jax.random.normal(ks[2], (E, D, F), jnp.float32) * w, 'w_up': jax.random.normal(ks[3], (E, D, F), jnp.float32) * w, 'w_down': jax.random.normal(ks[4], (E, F, D), jnp.float32) * w, 'ws_gate_up': jax.random.normal(ks[5], (D, 2 * SF), jnp.float32) * w, 'ws_down': jax.random.normal(ks[6], (SF, D), jnp.float32) * w}
    _L0_ffn_in = _L0_ffn_setup()
    _d = {'L0_attn_x': _L0_attn_in['x'], 'L0_attn_Wq': _L0_attn_in['Wq'], 'L0_attn_bq': _L0_attn_in['bq'], 'L0_attn_Wk': _L0_attn_in['Wk'], 'L0_attn_bk': _L0_attn_in['bk'], 'L0_attn_Wv': _L0_attn_in['Wv'], 'L0_attn_bv': _L0_attn_in['bv'], 'L0_attn_Wg1': _L0_attn_in['Wg1'], 'L0_attn_bg1': _L0_attn_in['bg1'], 'L0_attn_Wg2': _L0_attn_in['Wg2'], 'L0_attn_bg2': _L0_attn_in['bg2'], 'L0_ffn_router_w': _L0_ffn_in['router_w'], 'L0_ffn_w_gate': _L0_ffn_in['w_gate'], 'L0_ffn_w_up': _L0_ffn_in['w_up'], 'L0_ffn_w_down': _L0_ffn_in['w_down'], 'L0_ffn_ws_gate_up': _L0_ffn_in['ws_gate_up'], 'L0_ffn_ws_down': _L0_ffn_in['ws_down']}
    _x0 = _d['L0_attn_x']
    _d['L0_attn_x'] = jax.random.normal(jax.random.fold_in(jax.random.key(seed), 1), (2, 8192, 512), dtype=_x0.dtype)
    del _x0
    return _d

def reference(L0_attn_x, L0_attn_Wq, L0_attn_bq, L0_attn_Wk, L0_attn_bk, L0_attn_Wv, L0_attn_bv, L0_attn_Wg1, L0_attn_bg1, L0_attn_Wg2, L0_attn_bg2, L0_ffn_router_w, L0_ffn_w_gate, L0_ffn_w_up, L0_ffn_w_down, L0_ffn_ws_gate_up, L0_ffn_ws_down):

    def _L0_attn_ref(x, Wq, bq, Wk, bk, Wv, bv, Wg1, bg1, Wg2, bg2):
        import jax, jax.numpy as jnp
        import numpy as np
        DIM, H, C = (512, 16, 64)
        D = DIM // H
        GATE_HID = 16
        B, L, dim = x.shape
        pad = -L % C
        if pad:
            x = jnp.pad(x, ((0, 0), (0, pad), (0, 0)))
        Lp = L + pad

        def proj(W, b):
            return (x @ W + b).reshape(B, Lp, H, D).transpose(0, 2, 1, 3)
        q, k, v = (proj(Wq, bq), proj(Wk, bk), proj(Wv, bv))
        gate = jax.nn.sigmoid(jax.nn.silu(x @ Wg1 + bg1) @ Wg2 + bg2)
        alpha = 0.9 * gate.reshape(B, Lp, H, D).transpose(0, 2, 1, 3) + 0.1
        Nc = Lp // C
        qc = q.reshape(B, H, Nc, C, D)
        kc = k.reshape(B, H, Nc, C, D)
        vc = v.reshape(B, H, Nc, C, D)
        scores = jnp.einsum('bhncd,bhnkd->bhnck', qc, kc) / np.sqrt(D).astype(np.float32)
        causal = jnp.tril(jnp.ones((C, C), bool))
        scores = jnp.where(causal, scores, -jnp.inf)
        intra = jnp.einsum('bhnck,bhnke->bhnce', jax.nn.softmax(scores, axis=-1), vc)
        intra = intra.reshape(B, H, Lp, D)

        def step(S, inp):
            q_t, k_t, v_t, a_t = inp
            inter_t = jnp.einsum('bhd,bhde->bhe', q_t, S)
            S = a_t[..., None] * S + k_t[..., None] * v_t[..., None, :]
            return (S, inter_t)
        xs = tuple((a.transpose(2, 0, 1, 3) for a in (q, k, v, alpha)))
        S0 = jnp.zeros((B, H, D, D), x.dtype)
        _, inter = jax.lax.scan(step, S0, xs)
        inter = inter.transpose(1, 2, 0, 3)
        out = (inter + intra).transpose(0, 2, 1, 3).reshape(B, Lp, dim)
        return out[:, :L]

    def _L0_ffn_ref(hidden_states, router_w, w_gate, w_up, w_down, ws_gate_up, ws_down):
        import jax, jax.numpy as jnp
        import numpy as np
        B, S, D = (1, 1024, 512)
        E, K, F = (64, 8, 384)
        SF = 384
        C = 256
        ROUTED_SCALE = 1.0

        def _moe_forward(x, router_w, w_gate, w_up, w_down, ws_gate_up, ws_down):
            T = x.shape[0]
            logits = x.astype(jnp.float32) @ router_w.T
            probs = jax.nn.softmax(logits, axis=-1)
            topk_w, topk_ids = jax.lax.top_k(probs, K)
            topk_w = topk_w / jnp.sum(topk_w, axis=-1, keepdims=True)
            topk_w = topk_w.astype(x.dtype)
            N = T * K
            flat_e = topk_ids.reshape(-1)
            flat_w = topk_w.reshape(-1)
            tok = jnp.arange(N) // K
            onehot = flat_e[:, None] == jnp.arange(E)[None, :]
            pos = jnp.cumsum(onehot, axis=0)[jnp.arange(N), flat_e] - 1
            valid = pos < C
            idx = jnp.where(valid, flat_e * C + pos, E * C)
            x_buf = jnp.zeros((E * C + 1, x.shape[1]), x.dtype).at[idx].set(x[tok])
            xb = x_buf[:E * C].reshape(E, C, -1)
            g = jnp.einsum('ecd,edf->ecf', xb, w_gate)
            u = jnp.einsum('ecd,edf->ecf', xb, w_up)
            h = jax.nn.silu(g) * u
            y = jnp.einsum('ecf,efd->ecd', h, w_down).reshape(E * C, -1)
            safe = jnp.where(valid, idx, 0)
            contrib = y[safe] * (flat_w * valid.astype(flat_w.dtype))[:, None]
            routed = jax.ops.segment_sum(contrib, tok, num_segments=T)
            routed = routed * ROUTED_SCALE
            gu = x @ ws_gate_up
            sg, su = (gu[:, :SF], gu[:, SF:])
            shared = jax.nn.silu(sg) * su @ ws_down
            return routed + shared
        b, s, d = hidden_states.shape
        x = hidden_states.reshape(-1, d)
        out = _moe_forward(x, router_w, w_gate, w_up, w_down, ws_gate_up, ws_down)
        return out.reshape(b, s, d)
    x = L0_attn_x
    x = x + _L0_attn_ref(_layernorm(x, axis=-1), L0_attn_Wq, L0_attn_bq, L0_attn_Wk, L0_attn_bk, L0_attn_Wv, L0_attn_bv, L0_attn_Wg1, L0_attn_bg1, L0_attn_Wg2, L0_attn_bg2)
    x = x + _L0_ffn_ref(_layernorm(x, axis=-1), L0_ffn_router_w, L0_ffn_w_gate, L0_ffn_w_up, L0_ffn_w_down, L0_ffn_ws_gate_up, L0_ffn_ws_down)
    return x

_drawn_inputs = setup_inputs


def setup_inputs(seed=0):
    import zlib

    import numpy as np

    out = dict(_drawn_inputs(seed))
    spreads = {'L0_attn_bq': (0.0, 0.1),
     'L0_attn_bk': (0.0, 0.1),
     'L0_attn_bv': (0.0, 0.1),
     'L0_attn_bg1': (0.0, 0.8),
     'L0_attn_bg2': (0.0, 0.1)}
    factors = {'L0_ffn_router_w': 8.0,
     'L0_ffn_w_gate': 8.0,
     'L0_ffn_w_up': 8.0,
     'L0_ffn_w_down': 8.0,
     'L0_ffn_ws_gate_up': 8.0,
     'L0_ffn_ws_down': 8.0}
    for name, (base, spread) in spreads.items():
        noise = np.random.default_rng([zlib.crc32(name.encode()), seed]).standard_normal(out[name].shape)
        drawn = base * np.exp(spread * noise) if base else spread * noise
        out[name] = jnp.asarray(drawn.astype(out[name].dtype))
    for name, factor in factors.items():
        out[name] = (out[name] * factor).astype(out[name].dtype)
    return out
```

```python
import math
from contextlib import ExitStack

import concourse.bass as bass
from concourse import mybir

ACT = mybir.ActivationFunctionType
ALU = mybir.AluOpType
AX = mybir.AxisListType
f32, bf16, i32, u32 = mybir.dt.float32, mybir.dt.bfloat16, mybir.dt.int32, mybir.dt.uint32

P = 128
DIM = 512
KC = DIM // P
H, D = 16, 32
C = 64
HC = C // 2
GH = 16
BATCH, LEN = 2, 8192
NTOK = BATCH * LEN
TB = 256
NT = TB // P
NCH = TB // C
NBLK = NTOK // TB
E, TOPK, CAP = 64, 8, 256
F = 384
FC = F // P
SLOTS = E * CAP
ST = CAP // P
ROW = DIM + E
EPS = 1e-5
SCALE = 1.0 / math.sqrt(D)
NEG = -3.0e38
NOWHERE = 32768
GB = 4

JOBS = ["XTa", "XTb", "G1", "Qa", "G2a", "G2b", "Qb", "Ka", "Kb", "ATr0", "V0", "V1", "KTok0", "ATr1", "KTok1",
        "X2Ta", "X2Tb", "RL", "GU0", "RLT", "GU1", "DK0", "GU2", "DK1", "DN0", "DN1", "POS"]
PROJECT = ["XTa", "XTb", "G1", "Qa", "G2a", "G2b", "Qb", "Ka", "Kb", "V0", "V1", "KTok0", "KTok1", "DK0", "DK1"]


class Event:

    def __init__(self, sem, n, early):
        self.sem, self.n, self.early = sem, n, early

    def after(self, block, k):
        return self.early + self.n * block + k + 1


class Turn:

    def __init__(self, pair, odd):
        self.pair, self.odd = pair, odd

    def value(self, event, k=None, back=0):
        k = event.n - 1 if k is None else k
        return self.pair * (2 * event.n) + event.after(self.odd - back, k)

    def next(self, n=1):
        return Turn(self.pair, self.odd + n)

    @property
    def buf(self):
        return self.odd % 2


def layer_kernel(nc, x, Wq, bq, Wk, bk, Wv, bv, Wg1, bg1, Wg2, bg2, router_w, w_gate, w_up, w_down,
                 ws_gate_up, ws_down, out):
    x_rows = x.rearrange("b l d -> (b l) d").rearrange("(n t p) d -> n p t d", t=NT, p=P)
    out_flat = out.rearrange("b l d -> (b l) d")
    out_rows = out_flat.rearrange("(n t p) d -> n p t d", t=NT, p=P)
    norm_dram = nc.dram_tensor("norm_rows", (NTOK, ROW), f32, kind="Internal").ap()
    norm_rows = norm_dram.rearrange("(n t p) d -> n p t d", t=NT, p=P)
    table_dram = nc.dram_tensor("slot_tokens", (SLOTS, 1), i32, kind="Internal").ap()
    with nc.allow_non_contiguous_dma(reason="small weights and per-row pieces"):
        phase_tokens(nc, x_rows, Wq, bq, Wk, bk, Wv, bv, Wg1, bg1, Wg2, bg2, router_w,
                     ws_gate_up, ws_down, out_rows, norm_rows, table_dram)
        phase_experts(nc, w_gate, w_up, w_down, out_flat, norm_dram, table_dram)


def apart(engine, done):
    engine.sem_inc(done, 1)


def phase_tokens(nc, x_rows, Wq, bq, Wk, bk, Wv, bv, Wg1, bg1, Wg2, bg2, router_w, ws_gate_up,
                 ws_down, out_rows, norm_rows, table_dram):
    ctx = ExitStack()
    with ctx:
        def sb(name, shape, dt=f32):
            return ctx.enter_context(nc.sbuf_tensor(name, shape, dt))

        def sem(name):
            return ctx.enter_context(nc.semaphore(name))

        ident = sb("ident", [P, P])
        causal = sb("causal", [P, C])
        decay_mask = sb("decay_mask", [P, P])
        seg_start = sb("seg_start", [P, KC * TB])
        before = sb("before", [P, P], bf16)
        ones_b = sb("ones_b", [P, P], bf16)
        slot_base = sb("slot_base", [P, E])
        neg_half = sb("neg_half", [P, NT])
        keep = sb("keep", [P, NBLK + 1])
        wq = sb("wq", [P, KC, DIM])
        wk = sb("wk", [P, KC, DIM])
        wv = sb("wv", [P, KC, DIM])
        wg1 = sb("wg1", [P, KC, P])
        wg2 = sb("wg2", [P, DIM])
        wsgu = sb("wsgu", [P, KC, 2 * F])
        wsd = sb("wsd", [P, FC, DIM])
        rw = sb("rw", [E, DIM])
        rwT = sb("rwT", [P, KC, E])
        bq4 = sb("bq4", [P, KC])
        bk4 = sb("bk4", [P, KC])
        bvb = sb("bvb", [P, DIM])
        b1 = sb("b1", [P, 1])
        b1h = sb("b1h", [P, 1])
        b2 = sb("b2", [P, KC])
        b2h = sb("b2h", [P, KC])
        nowhere = sb("nowhere", [P, SLOTS // P], i32)
        X = [sb(f"X{i}", [P, NT, DIM]) for i in range(2)]
        st1 = sb("st1", [P, NT, 6])
        mv1 = sb("mv1", [P, NT, 2])
        ve1 = sb("ve1", [P, NT])
        rs1 = sb("rs1", [P, NT])
        XN = sb("XN", [P, NT, DIM])
        XT = sb("XT", [P, KC, TB])
        z1 = sb("z1", [P, TB])
        t1 = sb("t1", [P, TB])
        s1 = sb("s1", [P, TB])
        TH = sb("TH", [P, KC, TB])
        AL = sb("AL", [P, KC, TB])
        ALs = sb("ALs", [P, KC, TB])
        EX = sb("EX", [P, KC, TB])
        FI = sb("FI", [P, KC, TB])
        RF = sb("RF", [P, KC, TB])
        QT = [sb(f"QT{i}", [P, KC, TB]) for i in range(2)]
        KT = [sb(f"KT{i}", [P, KC, TB]) for i in range(2)]
        QD = [sb(f"QD{i}", [P, KC, TB]) for i in range(2)]
        KD = [sb(f"KD{i}", [P, KC, TB]) for i in range(2)]
        FS = [sb(f"FS{i}", [P, KC, NCH, 2]) for i in range(2)]
        V = [sb(f"V{i}", [P, NT, DIM]) for i in range(2)]
        V2 = [sb(f"V2{i}", [P, NT, DIM]) for i in range(2)]
        KTok = [sb(f"KTok{i}", [P, NT, DIM]) for i in range(2)]
        S = sb("S", [P, KC, D])
        U = sb("U", [P, KC, D])
        R = sb("R", [P, NCH, KC, D])
        SM = sb("SM", [P, 8, C])
        MX = sb("MX", [P, 8])
        PR = [sb(f"PR{i}", [P, 8, C]) for i in range(2)]
        SU = sb("SU", [P, 8])
        RU = sb("RU", [P, 8])
        AM = [sb(f"AM{i}", [P, 4, P]) for i in range(2)]
        WT = [sb(f"WT{i}", [P, 4, P]) for i in range(2)]
        OTs = [sb(f"OTs{i}", [P, KC, P]) for i in range(2)]
        X2 = sb("X2", [P, NT, DIM])
        st2 = sb("st2", [P, NT, 6])
        mv2 = sb("mv2", [P, NT, 2])
        ve2 = sb("ve2", [P, NT])
        rs2 = sb("rs2", [P, NT])
        XR = sb("XR", [P, NT, ROW])
        X2T = sb("X2T", [P, KC, TB])
        LT = sb("LT", [E, TB])
        LG = sb("LG", [P, NT, E])
        rmx = sb("rmx", [P, NT])
        PB = sb("PB", [P, NT, E])
        rsu = sb("rsu", [P, NT])
        rre = sb("rre", [P, NT])
        top = sb("top", [P, NT, 8])
        RP = sb("RP", [P, NT, E])
        M = sb("M", [P, NT, E], bf16)
        PW = sb("PW", [P, NT, E])
        PO = sb("PO", [P, NT, E])
        VA = sb("VA", [P, NT, E])
        T1 = sb("T1", [P, NT, E])
        T2 = sb("T2", [P, NT, E])
        carry = sb("carry", [P, E])
        key8 = sb("key8", [P, NT, 8])
        slot8 = sb("slot8", [P, NT, 8], i32)
        tokf = sb("tokf", [P, NT])
        toki = sb("toki", [P, NT], i32)
        TG = sb("TG", [P, TB])
        WG = sb("WG", [P, TB])
        HT = sb("HT", [P, FC, TB])
        OUT = sb("OUT", [P, NT, DIM])

        bank = [ctx.enter_context(nc.psum_tensor(f"bank{i}", [P, 512], f32)) for i in range(GB)]
        s_bank = ctx.enter_context(nc.psum_tensor("s_bank", [P, 512], f32))
        pt_bank = ctx.enter_context(nc.psum_tensor("pt_bank", [P, 512], f32))
        a_bank = ctx.enter_context(nc.psum_tensor("a_bank", [P, 512], f32))
        ot_bank = ctx.enter_context(nc.psum_tensor("ot_bank", [P, 512], f32))

        begun = sem("begun")
        consts_made = sem("consts_made")
        consts_done = sem("consts_done")
        gate_clear = sem("gate_clear")
        weights_in = sem("weights_in")
        table_clear = sem("table_clear")
        rw_turned = sem("rw_turned")
        rw_ready = sem("rw_ready")
        pool_chain = sem("pool_chain")
        pe_apart, dve_apart, pool_apart = sem("pe_apart"), sem("dve_apart"), sem("pool_apart")

        primed = []

        def event(name, n=1):
            primed.append(Event(sem(name), n, n))
            return primed[-1]

        x_loaded = event("x_loaded", 16)
        v_swapped = event("v_swapped", 32)
        rows_stored = event("rows_stored", 16)
        out_stored = event("out_stored", 16)
        scattered = Event(sem("scattered"), 16 * TOPK * NT, 0)
        slots_used = event("slots_used")
        var1_ready = event("var1_ready")
        rstd1_ready = event("rstd1_ready")
        xn_ready = event("xn_ready")
        xt_filled = event("xt_filled", 2)
        xt_ready = event("xt_ready", 2)
        g1_filled = event("g1_filled")
        g1_tanh = event("g1_tanh", 2)
        s1_ready = event("s1_ready")
        g2_filled = event("g2_filled", 2)
        th_ready = event("th_ready", 4)
        al_ready = event("al_ready")
        q_filled = event("q_filled", 2)
        q_ready = event("q_ready", 4)
        k_filled = event("k_filled", 2)
        k_ready = event("k_ready", 4)
        fs_ready = event("fs_ready")
        qd_ready = event("qd_ready")
        kd_ready = event("kd_ready")
        v_filled = event("v_filled", 2)
        v_ready = event("v_ready", 2)
        ktok_filled = event("ktok_filled", 2)
        ktok_ready = event("ktok_ready", 2)
        dk_filled = event("dk_filled", 2)
        r_ready = event("r_ready", 4)
        dk_used = event("dk_used", 2)
        s_rows = event("s_rows", 12)
        a_rows = event("a_rows", 12)
        s_filled = event("s_filled", 4)
        s_masked = event("s_masked", 4)
        a_filled = event("a_filled", 4)
        a_masked = event("a_masked", 4)
        shifted = event("shifted", 4)
        exped = event("exped", 4)
        p_ready = event("p_ready", 4)
        pt_filled = event("pt_filled", 4)
        w_ready = event("w_ready", 4)
        ot_filled = event("ot_filled", 4)
        ot_evac = event("ot_evac", 4)
        at_filled = event("at_filled", 2)
        x2_ready = event("x2_ready", 2)
        var2_ready = event("var2_ready", 2)
        rstd2_ready = event("rstd2_ready", 2)
        x2n_ready = event("x2n_ready", 2)
        x2t_filled = event("x2t_filled", 2)
        x2t_ready = event("x2t_ready", 2)
        rl_filled = event("rl_filled")
        lt_ready = event("lt_ready")
        rlt_filled = event("rlt_filled")
        logits_shifted = event("logits_shifted")
        router_exped = event("router_exped")
        m_ready = event("m_ready")
        rows_ready = event("rows_ready")
        pos_filled = event("pos_filled")
        pos_used = event("pos_used")
        slots_ready = event("slots_ready")
        gu_filled = event("gu_filled", 3)
        gu_tanh = event("gu_tanh", 3)
        gu_ready = event("gu_ready", 3)
        dn_filled = event("dn_filled", 2)
        out_ready = event("out_ready", 2)
        dve_chain = sem("dve_chain")

        READ = {"DK0": (dk_used, 0), "DK1": (dk_used, 1), "XTa": (xt_ready, 0), "XTb": (xt_ready, 1), "G1": (g1_tanh, 1),
                "Qa": (q_ready, 1), "Qb": (q_ready, 3), "G2a": (th_ready, 1), "G2b": (th_ready, 3),
                "Ka": (k_ready, 1), "Kb": (k_ready, 3), "ATr0": (x2_ready, 0), "ATr1": (x2_ready, 1),
                "V0": (v_ready, 0), "V1": (v_ready, 1), "KTok0": (ktok_ready, 0), "KTok1": (ktok_ready, 1),
                "X2Ta": (x2t_ready, 0), "X2Tb": (x2t_ready, 1), "RL": (lt_ready, 0),
                "RLT": (logits_shifted, 0), "POS": (pos_used, 0), "GU0": (gu_ready, 0),
                "GU1": (gu_ready, 1), "GU2": (gu_ready, 2), "DN0": (out_ready, 0), "DN1": (out_ready, 1)}

        def bank_of(job):
            return bank[JOBS.index(job) % GB]

        def heads(half, r=None):
            return [(4 * g + q, g, q) for g in (2 * half, 2 * half + 1) for q in range(4) if r in (None, q)]

        block = ctx.enter_context(nc.Block())

        @block.sync
        def _(sp):
            def load_x(t):
                sp.dma_start(X[t.buf][:, :, :], x_rows[t.pair * 2 + t.odd, :, :, :]).then_inc(x_loaded.sem, 16)

            sp.wait_ge(begun, 1)
            load_x(Turn(0, 0))
            for dst, src in ((wq, Wq), (wk, Wk), (wv, Wv), (wsgu, ws_gate_up), (wsd, ws_down)):
                sp.dma_start(dst[:, :, :], src.rearrange("(c p) n -> p c n", p=P)).then_inc(weights_in, 16)
            sp.wait_ge(gate_clear, 1)
            sp.dma_start(wg1[:, :, 0:GH], Wg1.rearrange("(c p) n -> p c n", p=P)).then_inc(weights_in, 16)
            sp.dma_start(wg2[0:GH, :], Wg2).then_inc(weights_in, 16)
            sp.dma_start(rw[:, :], router_w).then_inc(weights_in, 16)
            for dst, src in ((bq4, bq), (bk4, bk), (b2, bg2)):
                sp.dma_start(dst[:, :], src.rearrange("(c p) -> p c", p=P)).then_inc(weights_in, 16)
            sp.dma_start(b1[0:GH, :], bg1.rearrange("(p o) -> p o", o=1)).then_inc(weights_in, 16)
            sp.dma_start(bvb[:, :], bv.rearrange("(o n) -> o n", o=1).to_broadcast([P, DIM])).then_inc(weights_in, 16)
            load_x(Turn(0, 1))

            def swap_v(t):
                sp.wait_ge(v_ready.sem, t.value(v_ready))
                for a, b in ((0, C), (C, 0)):
                    sp.dma_start(V2[t.buf][a:a + C, :, :], V[t.buf][b:b + C, :, :]).then_inc(v_swapped.sem, 16)

            swap_v(Turn(0, 0))
            sp.wait_ge(consts_made, 1)
            sp.dma_start(table_dram.rearrange("(p c) o -> p (c o)", p=P), nowhere[:, :]).then_inc(table_clear, 16)

            def turn(t, last):
                sp.wait_ge(x2_ready.sem, t.value(x2_ready))
                if last:
                    sp.dma_start(X[t.buf][:, :, :], x_rows[0, :, :, :]).then_inc(x_loaded.sem, 16)
                else:
                    load_x(Turn(t.pair, t.odd + 2))
                swap_v(t.next())
                sp.wait_ge(rows_ready.sem, t.value(rows_ready))
                sp.dma_start(norm_rows[t.pair * 2 + t.odd, :, :, :], XR[:, :, :]).then_inc(rows_stored.sem, 16)
                sp.wait_ge(out_ready.sem, t.value(out_ready))
                sp.dma_start(out_rows[t.pair * 2 + t.odd, :, :, :], OUT[:, :, :]).then_inc(out_stored.sem, 16)

            with sp.Fori(0, NBLK // 2 - 1) as pair:
                for odd in range(2):
                    turn(Turn(pair, odd), False)
            end = NBLK // 2 - 1
            for odd in range(2):
                turn(Turn(end, odd), True)
            sp.wait_ge(x_loaded.sem, 16 * (NBLK + 3))
            sp.wait_ge(v_swapped.sem, 32 * (NBLK + 2))
            sp.wait_ge(rows_stored.sem, 16 * (NBLK + 1))
            sp.wait_ge(out_stored.sem, 16 * (NBLK + 1))

        @block.gpsimd
        def _(pool):
            links = [0]

            def link(ins):
                links[0] += 1
                ins.then_inc(pool_chain, 1)
                pool.wait_ge(pool_chain, links[0])

            for ev in primed:
                pool.sem_inc(ev.sem, ev.early)
            pool.sem_inc(begun, 1)
            nc.gpsimd.memset(wg1[:, :, :], 0.0)
            nc.gpsimd.memset(wg2[:, :], 0.0)
            nc.gpsimd.memset(b1[:, :], 0.0).then_inc(gate_clear, 1)
            link(nc.gpsimd.memset(nowhere[:, :], NOWHERE))
            link(nc.gpsimd.memset(ident[:, :], 0.0))
            link(nc.gpsimd.affine_select(out=ident[:, :], in_=ident[:, :], compare_op=ALU.not_equal, fill=1.0,
                                         base=0, pattern=[[-1, P]], channel_multiplier=1))
            link(nc.gpsimd.memset(causal[:, :], 0.0))
            for h in range(2):
                link(nc.gpsimd.affine_select(out=causal[h * C:(h + 1) * C, :], in_=causal[h * C:(h + 1) * C, :],
                                             compare_op=ALU.is_ge, fill=NEG, base=0, pattern=[[-1, C]],
                                             channel_multiplier=1))
            link(nc.gpsimd.memset(decay_mask[:, :], 1.0))
            for h in range(2):
                link(nc.gpsimd.affine_select(out=decay_mask[h * C:(h + 1) * C, :],
                                             in_=decay_mask[h * C:(h + 1) * C, :], compare_op=ALU.is_gt,
                                             fill=0.0, base=0, pattern=[[0, 2], [1, C]], channel_multiplier=-1))
            link(nc.gpsimd.memset(before[:, :], 1.0))
            link(nc.gpsimd.affine_select(out=before[:, :], in_=before[:, :], compare_op=ALU.is_gt, fill=0.0,
                                         base=0, pattern=[[1, P]], channel_multiplier=-1))
            link(nc.gpsimd.memset(ones_b[:, :], 1.0))
            link(nc.gpsimd.iota(slot_base[:, :], pattern=[[2, E]], base=0, channel_multiplier=0,
                                allow_small_or_imprecise_dtypes=True))
            link(nc.gpsimd.iota(tokf[:, :], pattern=[[P, NT]], base=0, channel_multiplier=1,
                                allow_small_or_imprecise_dtypes=True))
            link(nc.gpsimd.memset(seg_start[:, :], 0.0))
            link(nc.gpsimd.memset(seg_start[:, :].rearrange("p (s t) -> p s t", t=HC)[:, :, 0:1], 1.0))
            link(nc.gpsimd.memset(keep[:, :], 1.0))
            link(nc.gpsimd.memset(keep[:, 0:NBLK:NBLK // BATCH], 0.0))
            nc.gpsimd.memset(neg_half[:, :], -0.5).then_inc(consts_made, 1)
            pool.wait_ge(consts_made, 1)

            def rstd1(t):
                pool.wait_ge(var1_ready.sem, t.value(var1_ready))
                nc.gpsimd.tensor_tensor(rs1[:, :], ve1[:, :], neg_half[:, :], ALU.pow).then_inc(rstd1_ready.sem, 1)

            def rstd2(t, k):
                pool.wait_ge(var2_ready.sem, t.value(var2_ready, k))
                nc.gpsimd.tensor_tensor(rs2[:, k:k + 1], ve2[:, k:k + 1], neg_half[:, k:k + 1],
                                        ALU.pow).then_inc(rstd2_ready.sem, 1)

            def scatter(t):
                pool.wait_ge(slots_ready.sem, t.value(slots_ready))
                apart(pool, pool_apart)
                for tile in range(NT):
                    for k in range(TOPK):
                        nc.gpsimd.indirect_dma_start(
                            out=table_dram, out_offset=bass.IndirectOffsetOnAxis(ap=slot8[:, tile, k:k + 1], axis=0),
                            in_=toki[:, tile:tile + 1], in_offset=None, bounds_check=SLOTS - 1,
                            oob_is_err=False).then_inc(scattered.sem, 16)
                pool.wait_ge(scattered.sem, t.value(scattered))
                pool.sem_inc(slots_used.sem, 1)

            rstd1(Turn(0, 0))
            rstd1(Turn(0, 1))
            pool.wait_ge(table_clear, 16)
            with pool.Fori(0, NBLK // 2) as pair:
                for odd in range(2):
                    t = Turn(pair, odd)
                    for k in range(NT):
                        rstd2(t, k)
                    rstd1(t.next(2))
                    scatter(t)

        @block.scalar
        def _(act):
            def xt_evac(t):
                for k in range(2):
                    act.wait_ge(xt_filled.sem, t.value(xt_filled, k))
                    act.wait_ge(v_filled.sem, t.value(v_filled, back=1))
                    nc.scalar.activation(XT[:, 2 * k:2 * k + 2, :], bank_of("XTa" if k == 0 else "XTb")[:, :]
                                         .rearrange("p (a b) -> p a b", a=2), ACT.Copy).then_inc(xt_ready.sem, 1)

            def gate1(t):
                act.wait_ge(g1_filled.sem, t.value(g1_filled))
                act.wait_ge(s1_ready.sem, t.value(s1_ready, back=1))
                nc.scalar.activation(t1[:, :], bank_of("G1")[:, 0:TB], ACT.Tanh, bias=b1h[:, :], scale=0.5).then_inc(g1_tanh.sem, 1)
                nc.scalar.activation(z1[:, :], bank_of("G1")[:, 0:TB], ACT.Identity, bias=b1[:, :], scale=1.0).then_inc(g1_tanh.sem, 1)

            def gate2(t, k):
                act.wait_ge(g2_filled.sem, t.value(g2_filled, k))
                if k == 0:
                    act.wait_ge(fs_ready.sem, t.value(fs_ready, back=1))
                for m in (2 * k, 2 * k + 1):
                    nc.scalar.activation(TH[:, m, :], bank_of("G2a" if k == 0 else "G2b")[:, (m % 2) * TB:(m % 2 + 1) * TB],
                                         ACT.Tanh, bias=b2h[:, m:m + 1], scale=0.25).then_inc(th_ready.sem, 1)

            def alpha(t):
                act.wait_ge(th_ready.sem, t.value(th_ready))
                nc.scalar.activation(AL[:, :, :], TH[:, :, :], ACT.Copy, bias=0.55, scale=0.45).then_inc(al_ready.sem, 1)

            def qk_evac(t, k, filled, ready, dst, bias, names):
                act.wait_ge(filled.sem, t.value(filled, k))
                for m in (2 * k, 2 * k + 1):
                    nc.scalar.activation(dst[t.buf][:, m, :], bank_of(names[k])[:, (m % 2) * TB:(m % 2 + 1) * TB],
                                         ACT.Identity, bias=bias[:, m:m + 1], scale=1.0).then_inc(ready.sem, 1)

            def ktok_evac(t, k):
                act.wait_ge(ktok_filled.sem, t.value(ktok_filled, k))
                nc.scalar.activation(KTok[t.buf][:, k, :], bank_of(f"KTok{k}")[:, :], ACT.Copy).then_inc(ktok_ready.sem, 1)

            def exp(t, u):
                act.wait_ge(shifted.sem, t.value(shifted, u))
                nc.scalar.activation(PR[u % 2][:, :, :], PR[u % 2][:, :, :], ACT.Exp, scale=SCALE).then_inc(exped.sem, 1)

            def ot(t, u):
                act.wait_ge(ot_filled.sem, t.value(ot_filled, u))
                if u % 2 == 0:
                    act.wait_ge(at_filled.sem, t.value(at_filled, back=1))
                nc.scalar.activation(OTs[u // 2][:, 2 * (u % 2):2 * (u % 2) + 2, :],
                                     ot_bank[:, 0:2 * P].rearrange("p (a b) -> p a b", a=2),
                                     ACT.Copy).then_inc(ot_evac.sem, 1)

            def x2t(t):
                for k in range(2):
                    act.wait_ge(x2t_filled.sem, t.value(x2t_filled, k))
                    act.wait_ge(gu_filled.sem, t.value(gu_filled, back=1))
                    nc.scalar.activation(X2T[:, 2 * k:2 * k + 2, :], bank_of("X2Ta" if k == 0 else "X2Tb")[:, :]
                                         .rearrange("p (a b) -> p a b", a=2), ACT.Copy).then_inc(x2t_ready.sem, 1)

            def lt(t):
                act.wait_ge(rl_filled.sem, t.value(rl_filled))
                act.wait_ge(rlt_filled.sem, t.value(rlt_filled, back=1))
                nc.scalar.activation(LT[:, :], bank_of("RL")[0:E, 0:TB], ACT.Copy).then_inc(lt_ready.sem, 1)

            def router_exp(t):
                act.wait_ge(logits_shifted.sem, t.value(logits_shifted))
                nc.scalar.activation(PB[:, :, :], LG[:, :, :], ACT.Exp).then_inc(router_exped.sem, 1)

            def gu(t, m):
                act.wait_ge(gu_filled.sem, t.value(gu_filled, m))
                if m == 0:
                    act.wait_ge(gu_ready.sem, t.value(gu_ready, back=1))
                else:
                    act.wait_ge(gu_ready.sem, t.value(gu_ready, m - 1))
                nc.scalar.activation(TG[:, :], bank_of(f"GU{m}")[:, 0:TB], ACT.Tanh, scale=0.5).then_inc(gu_tanh.sem, 1)

            act.wait_ge(weights_in, 16 * 13)
            act.wait_ge(rw_turned, 1)
            nc.scalar.activation(rwT[:, :, :], bank[0][:, 0:KC * E].rearrange("p (a b) -> p a b", a=KC), ACT.Copy).then_inc(rw_ready, 1)
            nc.scalar.mul(b1h[:, :], b1[:, :], 0.5).then_inc(rw_ready, 1)
            nc.scalar.mul(b2h[:, :], b2[:, :], 0.5).then_inc(rw_ready, 1)
            act.wait_ge(rw_ready, 3)

            def q_evac(t, k):
                qk_evac(t, k, q_filled, q_ready, QT, bq4, ("Qa", "Qb"))

            def k_evac(t, k):
                qk_evac(t, k, k_filled, k_ready, KT, bk4, ("Ka", "Kb"))

            t = Turn(0, 0)
            xt_evac(t)
            gate1(t)
            q_evac(t, 0)
            for k in range(2):
                gate2(t, k)
            alpha(t)
            q_evac(t, 1)
            for k in range(2):
                k_evac(t, k)
            for k in range(2):
                ktok_evac(t, k)
            with act.Fori(0, NBLK // 2) as pair:
                for odd in range(2):
                    t = Turn(pair, odd)
                    n = t.next()
                    xt_evac(n)
                    exp(t, 0)
                    gate1(n)
                    exp(t, 1)
                    q_evac(n, 0)
                    gate2(n, 0)
                    gate2(n, 1)
                    ot(t, 0)
                    alpha(n)
                    exp(t, 2)
                    q_evac(n, 1)
                    ot(t, 1)
                    k_evac(n, 0)
                    exp(t, 3)
                    k_evac(n, 1)
                    ot(t, 2)
                    ot(t, 3)
                    ktok_evac(n, 0)
                    ktok_evac(n, 1)
                    x2t(t)
                    lt(t)
                    gu(t, 0)
                    router_exp(t)
                    gu(t, 1)
                    gu(t, 2)

        @block.tensor
        def _(pe):
            seen = []

            def take(job, t, jobs):
                at = jobs.index(job)
                mine = JOBS.index(job) % GB
                prior = [j for j in jobs[:at] if JOBS.index(j) % GB == mine]
                back = 0
                if not prior:
                    if jobs is PROJECT:
                        return bank_of(job)
                    prior = [j for j in jobs if JOBS.index(j) % GB == mine]
                    back = 1
                name = prior[-1]
                ev, k = READ[name]
                owner = t if (name not in PROJECT or jobs is PROJECT) else t.next()
                pe.wait_ge(ev.sem, owner.value(ev, k, back=back))
                return bank_of(job)

            def xt(t, k, jobs=JOBS):
                b = take("XTa" if k == 0 else "XTb", t, jobs)
                o = t if jobs is PROJECT else t.next()
                pe.wait_ge(xn_ready.sem, o.value(xn_ready))
                for a in range(2):
                    for tile in range(NT):
                        last = nc.tensor.transpose(b[:, a * TB + tile * P:a * TB + (tile + 1) * P],
                                                   XN[:, tile, (2 * k + a) * P:(2 * k + a + 1) * P], ident[:, :])
                last.then_inc(xt_filled.sem, 1)

            def gate1(t, jobs=JOBS):
                b = take("G1", t, jobs)
                o = t if jobs is PROJECT else t.next()
                pe.wait_ge(xt_ready.sem, o.value(xt_ready))
                for c in range(KC):
                    last = nc.tensor.matmul(b[:, 0:TB], wg1[:, c, :], XT[:, c, :], start=(c == 0), stop=(c == KC - 1))
                last.then_inc(g1_filled.sem, 1)

            def gate2(t, k, jobs=JOBS):
                b = take("G2a" if k == 0 else "G2b", t, jobs)
                o = t if jobs is PROJECT else t.next()
                pe.wait_ge(s1_ready.sem, o.value(s1_ready))
                for a in range(2):
                    m = 2 * k + a
                    last = nc.tensor.matmul(b[:, a * TB:(a + 1) * TB], wg2[:, m * P:(m + 1) * P], s1[:, :], start=True, stop=True)
                last.then_inc(g2_filled.sem, 1)

            def project(t, k, w, filled, names, jobs=JOBS, parts=(0, 1)):
                b = take(names[k], t, jobs) if 0 in parts else bank_of(names[k])
                for a in parts:
                    m = 2 * k + a
                    for c in range(KC):
                        last = nc.tensor.matmul(b[:, a * TB:(a + 1) * TB], w[:, c, m * P:(m + 1) * P], XT[:, c, :],
                                                start=(c == 0), stop=(c == KC - 1))
                if 1 in parts:
                    last.then_inc(filled.sem, 1)

            def values(t, tile, jobs=JOBS, chunks=range(KC)):
                b = take(f"V{tile}", t, jobs) if 0 in chunks else bank_of(f"V{tile}")
                for c in chunks:
                    last = nc.tensor.matmul(b[:, :], XT[:, c, tile * P:(tile + 1) * P], wv[:, c, :],
                                            start=(c == 0), stop=(c == KC - 1))
                if KC - 1 in chunks:
                    last.then_inc(v_filled.sem, 1)

            def ktok(t, tile, jobs=JOBS):
                b = take(f"KTok{tile}", t, jobs)
                o = t if jobs is PROJECT else t.next()
                pe.wait_ge(kd_ready.sem, o.value(kd_ready))
                for g in range(KC):
                    last = nc.tensor.transpose(b[:, g * P:(g + 1) * P], KD[o.buf][:, g, tile * P:(tile + 1) * P], ident[:, :])
                last.then_inc(ktok_filled.sem, 1)

            def state_updates(t, odd, jobs=JOBS):
                o = t if jobs is PROJECT else t.next()
                pe.wait_ge(ktok_ready.sem, o.value(ktok_ready))
                pe.wait_ge(v_ready.sem, o.value(v_ready))
                b = take(f"DK{odd}", t, jobs)
                apart(pe, pe_apart)
                rows = slice(C * odd, C * odd + C)
                for c in range(odd, NCH, 2):
                    for h in range(H):
                        g, r = divmod(h, 4)
                        col = (c // 2 * KC + g) * D
                        last = nc.tensor.matmul(b[D * r:D * r + D, col:col + D],
                                                KTok[o.buf][rows, c // 2, h * D:(h + 1) * D],
                                                V[o.buf][rows, c // 2, h * D:(h + 1) * D], start=True, stop=True)
                last.then_inc(dk_filled.sem, 1)

            def scores(t, u):
                tile, half = divmod(u, 2)
                if u == 0:
                    pe.wait_ge(qd_ready.sem, t.value(qd_ready))
                    pe.wait_ge(kd_ready.sem, t.value(kd_ready))
                pe.wait_ge(s_masked.sem, t.value(s_masked, u - 1))
                pe.wait_ge(a_masked.sem, t.value(a_masked, u - 1))
                q, k, qd, kd = QT[t.buf], KT[t.buf], QD[t.buf], KD[t.buf]
                for r in range(4):
                    rows = slice(D * r, D * r + D)
                    if r:
                        pe.wait_ge(s_rows.sem, t.value(s_rows, 3 * u + r - 1))
                    apart(pe, pe_apart)
                    for h, g, _ in heads(half, r):
                        n = h - 8 * half
                        for cc in range(2):
                            at = (2 * tile + cc) * C
                            for qh in range(2):
                                keys = HC * (qh + 1)
                                part = C * cc + HC * qh
                                last_s = nc.tensor.matmul(s_bank[part:part + HC, n * C:n * C + keys],
                                                          q[rows, g, at + HC * qh:at + HC * qh + HC],
                                                          k[rows, g, at:at + keys], start=True, stop=True)
                    if r == 3:
                        last_s.then_inc(s_filled.sem, 1)
                    else:
                        last_s.then_inc(s_rows.sem, 1)
                    if r:
                        pe.wait_ge(a_rows.sem, t.value(a_rows, 3 * u + r - 1))
                        apart(pe, pe_apart)
                    for h, g, _ in heads(half, r):
                        n = h - 8 * half
                        for cc in range(2):
                            at = (2 * tile + cc) * C
                            for kh in range(2):
                                part = C * (n % 2) + HC * kh
                                col = (n // 2) * P + C * cc
                                last_a = nc.tensor.matmul(a_bank[part:part + HC, col + HC * kh:col + C],
                                                          kd[rows, g, at + HC * kh:at + HC * kh + HC],
                                                          qd[rows, g, at + HC * kh:at + C], start=True, stop=True)
                    last_a.then_inc(a_filled.sem if r == 3 else a_rows.sem, 1)

            def turn_probs(t, u):
                pe.wait_ge(p_ready.sem, t.value(p_ready, u))
                pe.wait_ge(w_ready.sem, t.value(w_ready, u - 1) if u else t.value(w_ready, back=1))
                for hp in range(4):
                    last = nc.tensor.transpose(pt_bank[:, hp * P:(hp + 1) * P],
                                               PR[u % 2][:, 2 * hp:2 * hp + 2, :].rearrange("p a b -> p (a b)"), ident[:, :])
                last.then_inc(pt_filled.sem, 1)

            def outputs(t, u):
                tile, half = divmod(u, 2)
                pe.wait_ge(w_ready.sem, t.value(w_ready, u))
                if u == 0:
                    pe.wait_ge(v_swapped.sem, t.value(v_swapped))
                if u % 2 == 0:
                    pe.wait_ge(r_ready.sem, t.value(r_ready, 2 * tile + 1))
                pe.wait_ge(ot_evac.sem, t.value(ot_evac, u - 1))
                apart(pe, pe_apart)
                started = set()
                for h2 in range(2):
                    rows = slice(C * h2, C * h2 + C)
                    for h, g, r in heads(half):
                        if h % 2 != h2:
                            continue
                        for cc in range(2):
                            v = V[t.buf] if h2 == cc else V2[t.buf]
                            col = (g - 2 * half) * P + C * cc
                            nc.tensor.matmul(ot_bank[D * r:D * r + D, col:col + C], v[rows, tile, h * D:(h + 1) * D],
                                             WT[u % 2][rows, (h - 8 * half) // 2, C * cc:C * cc + C],
                                             start=r not in started, stop=False, skip_group_check=True)
                            started.add(r)
                for r in range(4):
                    for h, g, _ in heads(half, r):
                        for cc in range(2):
                            c = 2 * tile + cc
                            col = (g - 2 * half) * P + C * cc
                            last = nc.tensor.matmul(ot_bank[D * r:D * r + D, col:col + C], R[D * r:D * r + D, c, g, :],
                                                    QD[t.buf][D * r:D * r + D, g, c * C:(c + 1) * C],
                                                    start=False, stop=True, skip_group_check=True)
                last.then_inc(ot_filled.sem, 1)

            def turn_out(t, tile):
                b = take(f"ATr{tile}", t, JOBS)
                pe.wait_ge(ot_evac.sem, t.value(ot_evac, 2 * tile + 1))
                for g in range(KC):
                    last = nc.tensor.transpose(b[:, g * P:(g + 1) * P], OTs[tile][:, g, :], ident[:, :])
                last.then_inc(at_filled.sem, 1)

            def x2t(t, k):
                b = take("X2Ta" if k == 0 else "X2Tb", t, JOBS)
                pe.wait_ge(x2n_ready.sem, t.value(x2n_ready))
                for a in range(2):
                    for tile in range(NT):
                        last = nc.tensor.transpose(b[:, a * TB + tile * P:a * TB + (tile + 1) * P],
                                                   XR[:, tile, (2 * k + a) * P:(2 * k + a + 1) * P], ident[:, :])
                last.then_inc(x2t_filled.sem, 1)

            def router(t):
                b = take("RL", t, JOBS)
                pe.wait_ge(x2t_ready.sem, t.value(x2t_ready))
                for c in range(KC):
                    last = nc.tensor.matmul(b[0:E, 0:TB], rwT[:, c, :], X2T[:, c, :], start=(c == 0), stop=(c == KC - 1))
                last.then_inc(rl_filled.sem, 1)

            def turn_logits(t):
                b = take("RLT", t, JOBS)
                pe.wait_ge(lt_ready.sem, t.value(lt_ready))
                apart(pe, pe_apart)
                for tile in range(NT):
                    last = nc.tensor.transpose(b[:, tile * E:(tile + 1) * E], LT[:, tile * P:(tile + 1) * P], ident[0:E, 0:E])
                last.then_inc(rlt_filled.sem, 1)

            def positions(t):
                b = take("POS", t, JOBS)
                pe.wait_ge(m_ready.sem, t.value(m_ready))
                nc.tensor.matmul(b[:, 0:E], before[:, :], M[:, 0, :], start=True, stop=True)
                nc.tensor.matmul(b[:, E:2 * E], ones_b[:, :], M[:, 0, :], start=True, stop=False)
                nc.tensor.matmul(b[:, E:2 * E], before[:, :], M[:, 1, :], start=False, stop=True)
                nc.tensor.matmul(b[:, 2 * E:3 * E], ones_b[:, :], M[:, 0, :], start=True, stop=False)
                nc.tensor.matmul(b[:, 2 * E:3 * E], ones_b[:, :], M[:, 1, :], start=False, stop=True).then_inc(pos_filled.sem, 1)

            def gate_up(t, m):
                b = take(f"GU{m}", t, JOBS)
                for a in range(2):
                    for c in range(KC):
                        last = nc.tensor.matmul(b[:, a * TB:(a + 1) * TB], wsgu[:, c, a * F + m * P:a * F + (m + 1) * P],
                                                X2T[:, c, :], start=(c == 0), stop=(c == KC - 1))
                last.then_inc(gu_filled.sem, 1)

            def down(t, tile):
                b = take(f"DN{tile}", t, JOBS)
                pe.wait_ge(gu_ready.sem, t.value(gu_ready))
                for m in range(FC):
                    last = nc.tensor.matmul(b[:, :], HT[:, m, tile * P:(tile + 1) * P], wsd[:, m, :],
                                            start=(m == 0), stop=(m == FC - 1))
                last.then_inc(dn_filled.sem, 1)

            pe.wait_ge(consts_made, 1)
            pe.wait_ge(consts_done, 1)
            pe.wait_ge(weights_in, 16 * 13)
            for c in range(KC):
                last = nc.tensor.transpose(bank[0][:, c * E:(c + 1) * E], rw[:, c * P:(c + 1) * P], ident[0:E, 0:E])
            last.then_inc(rw_turned, 1)
            pe.wait_ge(rw_ready, 3)
            first = Turn(0, 0)
            for k in range(2):
                xt(first, k, PROJECT)
            gate1(first, PROJECT)
            project(first, 0, wq, q_filled, ("Qa", "Qb"), PROJECT)
            for k in range(2):
                gate2(first, k, PROJECT)
            project(first, 1, wq, q_filled, ("Qa", "Qb"), PROJECT)
            for k in range(2):
                project(first, k, wk, k_filled, ("Ka", "Kb"), PROJECT)
            for k in range(2):
                values(first, k, PROJECT)
            for k in range(2):
                ktok(first, k, PROJECT)
            pe.wait_ge(v_ready.sem, first.value(v_ready))
            pe.wait_ge(ktok_ready.sem, first.value(ktok_ready))
            for odd in range(2):
                state_updates(first, odd, PROJECT)
            pe.wait_ge(dk_used.sem, first.value(dk_used))
            with pe.Fori(0, NBLK // 2) as pair:
                for odd in range(2):
                    t = Turn(pair, odd)
                    xt(t, 0)
                    xt(t, 1)
                    scores(t, 0)
                    gate1(t)
                    project(t, 0, wq, q_filled, ("Qa", "Qb"), parts=(0,))
                    scores(t, 1)
                    project(t, 0, wq, q_filled, ("Qa", "Qb"), parts=(1,))
                    turn_probs(t, 0)
                    gate2(t, 0)
                    gate2(t, 1)
                    outputs(t, 0)
                    project(t, 1, wq, q_filled, ("Qa", "Qb"), parts=(0,))
                    turn_probs(t, 1)
                    scores(t, 2)
                    project(t, 1, wq, q_filled, ("Qa", "Qb"), parts=(1,))
                    outputs(t, 1)
                    project(t, 0, wk, k_filled, ("Ka", "Kb"))
                    project(t, 1, wk, k_filled, ("Ka", "Kb"), parts=(0,))
                    turn_probs(t, 2)
                    turn_out(t, 0)
                    scores(t, 3)
                    project(t, 1, wk, k_filled, ("Ka", "Kb"), parts=(1,))
                    outputs(t, 2)
                    values(t, 0)
                    turn_probs(t, 3)
                    values(t, 1, chunks=(0, 1))
                    outputs(t, 3)
                    ktok(t, 0)
                    turn_out(t, 1)
                    values(t, 1, chunks=(2, 3))
                    ktok(t, 1)
                    x2t(t, 0)
                    x2t(t, 1)
                    router(t)
                    gate_up(t, 0)
                    turn_logits(t)
                    gate_up(t, 1)
                    state_updates(t, 0)
                    gate_up(t, 2)
                    state_updates(t, 1)
                    down(t, 0)
                    down(t, 1)
                    positions(t)

        @block.vector
        def _(dve):
            LINKS = 53
            links = [0, None]

            def link(ins):
                ins.then_inc(dve_chain, 1)
                links[0] += 1
                t = links[1]
                dve.wait_ge(dve_chain, links[0] if t is None else t.pair * (2 * LINKS) + (START + t.odd * LINKS + links[0]))

            v = nc.vector

            def bc(ap, n):
                return ap.unsqueeze(2).to_broadcast([ap.shape[0], ap.shape[1], n])

            def mid(ap, n):
                return ap.unsqueeze(1).to_broadcast([ap.shape[0], n, ap.shape[1]])

            def segs(ap):
                return ap.rearrange("p c (s t) -> p (c s) t", t=HC)

            def norm1(t):
                dve.wait_ge(x_loaded.sem, t.value(x_loaded))
                for k in range(NT):
                    ins = v.bn_stats(st1[:, k, :], X[t.buf][:, k, :])
                link(ins)
                apart(dve, dve_apart)
                for k in range(NT):
                    ins = v.bn_aggr(mv1[:, k, :], st1[:, k, :])
                link(ins)
                v.tensor_scalar(ve1[:, :], mv1[:, :, 1], EPS, None, ALU.add).then_inc(var1_ready.sem, 1)

            def norm1b(t):
                dve.wait_ge(rstd1_ready.sem, t.value(rstd1_ready))
                dve.wait_ge(xt_filled.sem, t.value(xt_filled, back=1))
                for k in range(NT):
                    ins = v.tensor_scalar(XN[:, k, :], X[t.buf][:, k, :], mv1[:, k, 0:1], rs1[:, k:k + 1],
                                          ALU.subtract, ALU.mult)
                ins.then_inc(xn_ready.sem, 1)

            def silu1(t):
                dve.wait_ge(g1_tanh.sem, t.value(g1_tanh))
                dve.wait_ge(g2_filled.sem, t.value(g2_filled, back=1))
                v.scalar_tensor_tensor(s1[:, :], t1[:, :], 1.0, z1[:, :], ALU.add, ALU.mult).then_inc(s1_ready.sem, 1)

            def decays(t):
                dve.wait_ge(th_ready.sem, t.value(th_ready))
                link(v.tensor_scalar(segs(ALs[:, :, :])[:, :, 1:HC], segs(TH[:, :, :])[:, :, 0:HC - 1], 0.45, 0.55,
                                     ALU.mult, ALU.add))
                link(v.tensor_tensor_scan(EX[:, :, :].rearrange("p c t -> p (c t)"), ALs[:, :, :].rearrange("p c t -> p (c t)"),
                                          seg_start[:, :], 0.0, ALU.mult, ALU.add))
                dve.wait_ge(al_ready.sem, t.value(al_ready))
                link(v.tensor_tensor(FI[:, :, :], EX[:, :, :], AL[:, :, :], ALU.mult))

            def products(t):
                v.tensor_copy(FS[t.buf][:, :, :, :].rearrange("p c n a -> p (c n a)"),
                              segs(FI[:, :, :])[:, :, HC - 1]).then_inc(fs_ready.sem, 1)
                dve.wait_ge(fs_ready.sem, t.value(fs_ready))

            def inverse(t, m):
                link(v.reciprocal(RF[:, m, :], FI[:, m, :]))

            def decayed_q(t):
                dve.wait_ge(q_ready.sem, t.value(q_ready))
                link(v.tensor_tensor(QD[t.buf][:, :, :], QT[t.buf][:, :, :], EX[:, :, :], ALU.mult))
                first = QD[t.buf][:, :, :].rearrange("p c (n s) -> p (c n) s", s=C)[:, :, 0:HC]
                r = RF[:, :, :].rearrange("p c (n s) -> p (c n) s", s=C)[:, :, HC - 1]
                v.tensor_tensor(first, first, bc(r, HC), ALU.mult).then_inc(qd_ready.sem, 1)

            def decayed_k(t):
                dve.wait_ge(k_ready.sem, t.value(k_ready))
                link(v.tensor_tensor(KD[t.buf][:, :, :], KT[t.buf][:, :, :], RF[:, :, :], ALU.mult))
                first = KD[t.buf][:, :, :].rearrange("p c (n s) -> p (c n) s", s=C)[:, :, 0:HC]
                m = FS[t.buf][:, :, :, 0].rearrange("p c n -> p (c n)")
                v.tensor_tensor(first, first, bc(m, HC), ALU.mult).then_inc(kd_ready.sem, 1)

            def values(t, k):
                dve.wait_ge(v_filled.sem, t.value(v_filled, k))
                v.tensor_tensor(V[t.buf][:, k, :], bank_of(f"V{k}")[:, :], bvb[:, :], ALU.add).then_inc(v_ready.sem, 1)

            def state(t):
                dve.wait_ge(dk_filled.sem, t.value(dk_filled))
                dve.wait_ge(ot_filled.sem, t.value(ot_filled, back=1))
                for c in range(NCH):
                    mid_f, end_f = FS[t.buf][:, :, c, 0], FS[t.buf][:, :, c, 1]
                    if c == 0:
                        ins = v.scalar_tensor_tensor(R[:, c, :, :], S[:, :, :], keep[:, bass.ds(t.pair * 2 + t.odd, 1)],
                                                     bc(mid_f, D), ALU.mult, ALU.mult)
                    else:
                        ins = v.tensor_tensor(R[:, c, :, :], S[:, :, :], bc(mid_f, D), ALU.mult)
                    ins.then_inc(r_ready.sem, 1)
                    dve.wait_ge(r_ready.sem, t.value(r_ready, c))
                    dk = bank_of(f"DK{c % 2}")[:, c // 2 * P:(c // 2 + 1) * P].rearrange("p (g e) -> p g e", g=KC)
                    ins = v.tensor_tensor(U[:, :, :], R[:, c, :, :], dk, ALU.add)
                    if c >= NCH - 2:
                        ins.then_inc(dk_used.sem, 1)
                        dve.wait_ge(dk_used.sem, t.value(dk_used, c % 2))
                    else:
                        link(ins)
                    link(v.tensor_tensor(S[:, :, :], U[:, :, :], bc(end_f, D), ALU.mult))

            def softmax_a(t, u):
                dve.wait_ge(s_filled.sem, t.value(s_filled, u))
                v.tensor_tensor(SM[:, :, :], s_bank[:, :].rearrange("p (n k) -> p n k", k=C), mid(causal[:, :], 8),
                                ALU.add).then_inc(s_masked.sem, 1)
                dve.wait_ge(s_masked.sem, t.value(s_masked, u))
                link(v.tensor_reduce(MX[:, :], SM[:, :, :], AX.X, ALU.max))
                if u >= 2:
                    dve.wait_ge(pt_filled.sem, t.value(pt_filled, u - 2))
                else:
                    dve.wait_ge(pt_filled.sem, t.value(pt_filled, back=1))
                v.tensor_tensor(PR[u % 2][:, :, :], SM[:, :, :], bc(MX[:, :], C), ALU.subtract).then_inc(shifted.sem, 1)
                dve.wait_ge(a_filled.sem, t.value(a_filled, u))
                v.tensor_tensor(AM[u % 2][:, :, :], a_bank[:, :].rearrange("p (n k) -> p n k", k=P),
                                mid(decay_mask[:, :], 4), ALU.mult).then_inc(a_masked.sem, 1)

            def softmax_b(t, u):
                dve.wait_ge(exped.sem, t.value(exped, u))
                link(v.tensor_reduce(SU[:, :], PR[u % 2][:, :, :], AX.X, ALU.add))
                link(v.reciprocal(RU[:, :], SU[:, :]))
                v.tensor_tensor(PR[u % 2][:, :, :], PR[u % 2][:, :, :], bc(RU[:, :], C), ALU.mult).then_inc(p_ready.sem, 1)

            def weights(t, u):
                dve.wait_ge(pt_filled.sem, t.value(pt_filled, u))
                dve.wait_ge(a_masked.sem, t.value(a_masked, u))
                if u >= 2:
                    dve.wait_ge(ot_filled.sem, t.value(ot_filled, u - 2))
                else:
                    dve.wait_ge(ot_filled.sem, t.value(ot_filled, back=1))
                v.tensor_tensor(WT[u % 2][:, :, :], pt_bank[:, :].rearrange("p (n k) -> p n k", k=P), AM[u % 2][:, :, :],
                                ALU.add).then_inc(w_ready.sem, 1)

            def residual(t, k):
                dve.wait_ge(at_filled.sem, t.value(at_filled, k))
                v.tensor_tensor(X2[:, k, :], bank_of(f"ATr{k}")[:, :], X[t.buf][:, k, :], ALU.add).then_inc(x2_ready.sem, 1)
                dve.wait_ge(x2_ready.sem, t.value(x2_ready, k))
                link(v.bn_stats(st2[:, k, :], X2[:, k, :]))
                apart(dve, dve_apart)
                link(v.bn_aggr(mv2[:, k, :], st2[:, k, :]))
                v.tensor_scalar(ve2[:, k:k + 1], mv2[:, k, 1:2], EPS, None, ALU.add).then_inc(var2_ready.sem, 1)

            def norm2(t, k):
                dve.wait_ge(rstd2_ready.sem, t.value(rstd2_ready, k))
                if k == 0:
                    dve.wait_ge(rows_stored.sem, t.value(rows_stored, back=1))
                    dve.wait_ge(x2t_filled.sem, t.value(x2t_filled, back=1))
                v.tensor_scalar(XR[:, k, 0:DIM], X2[:, k, :], mv2[:, k, 0:1], rs2[:, k:k + 1],
                                ALU.subtract, ALU.mult).then_inc(x2n_ready.sem, 1)

            def route_a(t):
                dve.wait_ge(rlt_filled.sem, t.value(rlt_filled))
                lg = bank_of("RLT")[:, 0:NT * E].rearrange("p (a b) -> p a b", a=NT)
                link(v.tensor_reduce(rmx[:, :], lg, AX.X, ALU.max))
                v.tensor_tensor(LG[:, :, :], lg, bc(rmx[:, :], E), ALU.subtract).then_inc(logits_shifted.sem, 1)

            def route_b(t):
                dve.wait_ge(router_exped.sem, t.value(router_exped))
                link(v.tensor_reduce(rsu[:, :], PB[:, :, :], AX.X, ALU.add))
                link(v.reciprocal(rre[:, :], rsu[:, :]))
                link(v.tensor_tensor(PB[:, :, :], PB[:, :, :], bc(rre[:, :], E), ALU.mult))
                apart(dve, dve_apart)
                for k in range(NT):
                    ins = v.max(top[:, k, :], PB[:, k, :])
                link(ins)
                apart(dve, dve_apart)
                for k in range(NT):
                    ins = v.match_replace(RP[:, k, :], top[:, k, :], PB[:, k, :], -1.0)
                link(ins)
                dve.wait_ge(pos_filled.sem, t.value(pos_filled, back=1))
                v.tensor_tensor(M[:, :, :], RP[:, :, :], PB[:, :, :], ALU.is_lt).then_inc(m_ready.sem, 1)
                dve.wait_ge(m_ready.sem, t.value(m_ready))
                link(v.tensor_tensor(PW[:, :, :], PB[:, :, :], M[:, :, :], ALU.mult))
                link(v.tensor_reduce(rsu[:, :], PW[:, :, :], AX.X, ALU.add))
                link(v.reciprocal(rre[:, :], rsu[:, :]))
                v.tensor_tensor(XR[:, :, DIM:ROW], PW[:, :, :], bc(rre[:, :], E), ALU.mult).then_inc(rows_ready.sem, 1)

            def route_c(t):
                dve.wait_ge(pos_filled.sem, t.value(pos_filled))
                b = bank_of("POS")
                link(v.tensor_tensor(PO[:, :, :], b[:, 0:NT * E].rearrange("p (a b) -> p a b", a=NT), mid(carry[:, :], NT), ALU.add))
                v.tensor_tensor(carry[:, :], carry[:, :], b[:, NT * E:(NT + 1) * E], ALU.add).then_inc(pos_used.sem, 1)
                v.scalar_tensor_tensor(VA[:, :, :], PO[:, :, :], float(CAP), M[:, :, :], ALU.is_lt, ALU.mult)
                link(v.tensor_scalar(T1[:, :, :], PO[:, :, :], float(P), float(P * P - 1), ALU.is_ge, ALU.mult))
                link(v.scalar_tensor_tensor(T2[:, :, :], PO[:, :, :], float(P), T1[:, :, :], ALU.mult, ALU.subtract))
                link(v.tensor_tensor(T1[:, :, :], T2[:, :, :], mid(slot_base[:, :], NT), ALU.add))
                link(v.tensor_scalar(T2[:, :, :], T1[:, :, :], -1.0, float(NOWHERE), ALU.mult, ALU.add))
                link(v.tensor_tensor(T1[:, :, :], T2[:, :, :], VA[:, :, :], ALU.mult))
                apart(dve, dve_apart)
                for k in range(NT):
                    ins = v.max(key8[:, k, :], T1[:, k, :])
                link(ins)
                dve.wait_ge(slots_used.sem, t.value(slots_used, back=1))
                v.tensor_copy(toki[:, :], tokf[:, :])
                v.tensor_scalar(slot8[:, :, :], key8[:, :, :], -1.0, float(NOWHERE), ALU.mult, ALU.add).then_inc(slots_ready.sem, 1)
                dve.wait_ge(slots_ready.sem, t.value(slots_ready))
                link(v.tensor_scalar(tokf[:, :], tokf[:, :], float(TB), None, ALU.add))

            def hidden(t, m):
                dve.wait_ge(gu_tanh.sem, t.value(gu_tanh, m))
                b = bank_of(f"GU{m}")
                link(v.scalar_tensor_tensor(WG[:, :], TG[:, :], 1.0, b[:, 0:TB], ALU.add, ALU.mult))
                if m == 0:
                    dve.wait_ge(dn_filled.sem, t.value(dn_filled, back=1))
                v.scalar_tensor_tensor(HT[:, m, :], WG[:, :], 0.5, b[:, TB:2 * TB], ALU.mult, ALU.mult).then_inc(gu_ready.sem, 1)
                dve.wait_ge(gu_ready.sem, t.value(gu_ready, m))

            def total(t, k):
                dve.wait_ge(dn_filled.sem, t.value(dn_filled, k))
                if k == 0:
                    dve.wait_ge(out_stored.sem, t.value(out_stored, back=1))
                v.tensor_tensor(OUT[:, k, :], bank_of(f"DN{k}")[:, :], X2[:, k, :], ALU.add).then_inc(out_ready.sem, 1)

            v.memset(s_bank[:, :], 0.0)
            v.memset(a_bank[:, :], 0.0)
            v.memset(carry[:, :], 0.0)
            v.memset(S[:, :, :], 0.0)
            v.memset(ALs[:, :, :], 0.0).then_inc(consts_done, 1)
            dve.wait_ge(consts_done, 1)
            dve.wait_ge(consts_made, 1)
            dve.wait_ge(weights_in, 16 * 13)
            t = Turn(0, 0)
            norm1(t)
            norm1b(t)
            silu1(t)
            decays(t)
            products(t)
            for m in range(KC):
                inverse(t, m)
            decayed_q(t)
            decayed_k(t)
            for k in range(NT):
                values(t, k)
            norm1(t.next())
            norm1b(t.next())
            state(t)
            START = links[0]
            with dve.Fori(0, NBLK // 2) as pair:
                for odd in range(2):
                    t = Turn(pair, odd)
                    n = t.next()
                    links[0], links[1] = 0, t
                    softmax_a(t, 0)
                    silu1(n)
                    softmax_b(t, 0)
                    softmax_a(t, 1)
                    weights(t, 0)
                    softmax_b(t, 1)
                    decays(n)
                    products(n)
                    weights(t, 1)
                    softmax_a(t, 2)
                    inverse(n, 0)
                    softmax_b(t, 2)
                    inverse(n, 1)
                    inverse(n, 2)
                    weights(t, 2)
                    residual(t, 0)
                    softmax_a(t, 3)
                    inverse(n, 3)
                    softmax_b(t, 3)
                    norm2(t, 0)
                    decayed_q(n)
                    values(n, 0)
                    weights(t, 3)
                    decayed_k(n)
                    residual(t, 1)
                    norm2(t, 1)
                    values(n, 1)
                    hidden(t, 0)
                    norm1(t.next(2))
                    route_a(t)
                    norm1b(t.next(2))
                    hidden(t, 1)
                    route_b(t)
                    hidden(t, 2)
                    state(n)
                    total(t, 0)
                    total(t, 1)
                    route_c(t)
                    assert links[0] == LINKS, links[0]


def phase_experts(nc, w_gate, w_up, w_down, out_flat, norm_dram, table_dram):
    ctx = ExitStack()
    with ctx:
        def sb(name, shape, dt=f32):
            return ctx.enter_context(nc.sbuf_tensor(name, shape, dt))

        def sem(name):
            return ctx.enter_context(nc.semaphore(name))

        ident = sb("ident2", [P, P])
        tokens = sb("tokens", [P, ST * (E + 2)], i32)
        WGt = [sb(f"WGt{i}", [P, KC, F]) for i in range(2)]
        WUp = [sb(f"WUp{i}", [P, KC, F]) for i in range(2)]
        WDn = [sb(f"WDn{i}", [P, FC, DIM]) for i in range(2)]
        XG = [sb(f"XG{i}", [P, ST, ROW + 1]) for i in range(2)]
        XE = [sb(f"XE{i}", [P, KC, CAP]) for i in range(2)]
        row_at = [sb(f"row_at{i}", [P, ST], i32) for i in range(2)]
        sum_at = sb("sum_at", [P, ST], i32)
        WC = [sb(f"WC{i}", [P, ST]) for i in range(2)]
        OG = sb("OG", [P, ST, DIM])
        TG = sb("TGe", [P, CAP])
        WG = sb("WGe", [P, CAP])
        HT = sb("HTe", [P, FC, CAP])
        bank = [ctx.enter_context(nc.psum_tensor(f"ebank{i}", [P, 512], f32)) for i in range(7)]
        TURN, HID, DOWN = (0, 1), (2, 3, 4), (5, 6)

        primed = []

        def event(name, n=1):
            primed.append(Event(sem(name), n, n))
            return primed[-1]

        ident_made = sem("ident_made")
        table_in = sem("table_in")
        pool_apart = sem("pool_apart2")
        cleared = sem("cleared")
        begun = sem("begun2")
        w_in = [sem(f"expert_weights_in{i}") for i in range(2)]
        row_at_ready = event("row_at_ready")
        sum_at_ready = event("sum_at_ready")
        wc_ready = event("wc_ready")
        gathered = [sem(f"rows_gathered{i}") for i in range(2)]
        sums_in = Event(sem("sums_gathered"), 16 * ST, 0)
        sums_out = Event(sem("sums_scattered"), 16 * ST, 0)
        xe_filled = event("xe_filled", 2)
        xe_ready = event("xe_ready", 2)
        gu_filled = event("e_gu_filled", 3)
        gu_tanh = event("e_gu_tanh", 3)
        gu_ready = event("e_gu_ready", 3)
        dn_filled = event("e_dn_filled", 2)
        sum_ready = event("sum_ready", 2)

        block = ctx.enter_context(nc.Block())

        @block.sync
        def _(sp):
            sp.wait_ge(begun, 1)
            sp.dma_start(tokens[:, 0:ST * E], table_dram.rearrange("(p c) o -> p (c o)", p=P)).then_inc(table_in, 16)

            def load(t):
                e = t.pair * 2 + t.odd
                ws = (WGt, WUp, WDn)
                for w, src in zip(ws, (w_gate, w_up, w_down)):
                    sp.dma_start(w[t.buf][:, :, :], src.rearrange("e (c p) n -> e p c n", p=P)[e, :, :, :]).then_inc(w_in[t.buf], 16)

            for odd in range(2):
                load(Turn(0, odd))
            with sp.Fori(0, E // 2 - 1) as pair:
                for odd in range(2):
                    t = Turn(pair, odd)
                    sp.wait_ge(dn_filled.sem, t.value(dn_filled))
                    load(Turn(pair, odd + 2))
            for i in range(2):
                sp.wait_ge(w_in[i], 48 * (E // 2))

        @block.gpsimd
        def _(pool):
            for ev in primed:
                pool.sem_inc(ev.sem, ev.early)
            pool.sem_inc(begun, 1)
            nc.gpsimd.memset(ident[:, :], 0.0).then_inc(ident_made, 1)
            pool.wait_ge(ident_made, 1)
            nc.gpsimd.affine_select(out=ident[:, :], in_=ident[:, :], compare_op=ALU.not_equal, fill=1.0,
                                    base=0, pattern=[[-1, P]], channel_multiplier=1).then_inc(ident_made, 1)
            pool.wait_ge(table_in, 16)
            pool.wait_ge(cleared, 1)

            def gather_rows(t):
                nc.gpsimd.tensor_copy(row_at[t.buf][:, :], tokens[:, bass.ds(t.pair * (2 * ST) + t.odd * ST, ST)]).then_inc(row_at_ready.sem, 1)
                pool.wait_ge(row_at_ready.sem, t.value(row_at_ready))
                apart(pool, pool_apart)
                for k in range(ST):
                    nc.gpsimd.indirect_dma_start(
                        out=XG[t.buf][:, k, 0:ROW], out_offset=None, in_=norm_dram,
                        in_offset=bass.IndirectOffsetOnAxis(ap=row_at[t.buf][:, k:k + 1], axis=0), bounds_check=NTOK - 1,
                        oob_is_err=False).then_inc(gathered[t.buf], 16)

            def gather_sums(t):
                nc.gpsimd.tensor_copy(sum_at[:, :], tokens[:, bass.ds(t.pair * (2 * ST) + t.odd * ST, ST)]).then_inc(sum_at_ready.sem, 1)
                pool.wait_ge(sum_at_ready.sem, t.value(sum_at_ready))
                apart(pool, pool_apart)
                for k in range(ST):
                    nc.gpsimd.indirect_dma_start(
                        out=OG[:, k, :], out_offset=None, in_=out_flat,
                        in_offset=bass.IndirectOffsetOnAxis(ap=sum_at[:, k:k + 1], axis=0), bounds_check=NTOK - 1,
                        oob_is_err=False).then_inc(sums_in.sem, 16)

            def store_sums(t):
                for k in range(ST):
                    pool.wait_ge(sum_ready.sem, t.value(sum_ready, k))
                    apart(pool, pool_apart)
                    nc.gpsimd.indirect_dma_start(
                        out=out_flat, out_offset=bass.IndirectOffsetOnAxis(ap=sum_at[:, k:k + 1], axis=0),
                        in_=OG[:, k, :], in_offset=None, bounds_check=NTOK - 1,
                        oob_is_err=False).then_inc(sums_out.sem, 16)
                pool.wait_ge(sums_out.sem, t.value(sums_out))

            gather_rows(Turn(0, 0))
            gather_rows(Turn(0, 1))
            with pool.Fori(0, E // 2) as pair:
                for odd in range(2):
                    t = Turn(pair, odd)
                    pool.wait_ge(xe_filled.sem, t.value(xe_filled))
                    pool.wait_ge(wc_ready.sem, t.value(wc_ready))
                    pool.wait_ge(gathered[t.buf], t.pair * (16 * ST) + 16 * ST)
                    gather_rows(Turn(pair, odd + 2))
                    gather_sums(t)
                    store_sums(t)
            pool.wait_ge(gathered[0], 16 * ST * (E // 2 + 1))
            pool.wait_ge(gathered[1], 16 * ST * (E // 2 + 1))

        @block.scalar
        def _(act):
            def xe(t):
                for k in range(ST):
                    act.wait_ge(xe_filled.sem, t.value(xe_filled, k))
                    nc.scalar.activation(XE[t.buf][:, :, k * P:(k + 1) * P], bank[TURN[k]][:, :].rearrange("p (c s) -> p c s", c=KC),
                                         ACT.Copy).then_inc(xe_ready.sem, 1)

            xe(Turn(0, 0))
            with act.Fori(0, E // 2) as pair:
                for odd in range(2):
                    t = Turn(pair, odd)
                    for m in range(FC):
                        act.wait_ge(gu_filled.sem, t.value(gu_filled, m))
                        act.wait_ge(gu_ready.sem, t.value(gu_ready, m - 1) if m else t.value(gu_ready, back=1))
                        nc.scalar.activation(TG[:, :], bank[HID[m]][:, 0:CAP], ACT.Tanh, scale=0.5).then_inc(gu_tanh.sem, 1)
                    xe(t.next())

        @block.tensor
        def _(pe):
            pe.wait_ge(ident_made, 2)

            def turn_rows(t):
                for k in range(ST):
                    pe.wait_ge(gathered[t.buf], t.pair * (16 * ST) + 16 * ST * (t.odd // 2 + 1))
                    pe.wait_ge(xe_ready.sem, t.value(xe_ready, k, back=1))
                    for c in range(KC):
                        last = nc.tensor.transpose(bank[TURN[k]][:, c * P:(c + 1) * P], XG[t.buf][:, k, c * P:(c + 1) * P], ident[:, :])
                    last.then_inc(xe_filled.sem, 1)

            turn_rows(Turn(0, 0))
            with pe.Fori(0, E // 2) as pair:
                for odd in range(2):
                    t = Turn(pair, odd)
                    pe.wait_ge(w_in[odd], pair * 48 + 48)
                    pe.wait_ge(xe_ready.sem, t.value(xe_ready))
                    for m in range(FC):
                        pe.wait_ge(gu_ready.sem, t.value(gu_ready, m, back=1))
                        for a, w in enumerate((WGt[odd], WUp[odd])):
                            for c in range(KC):
                                last = nc.tensor.matmul(bank[HID[m]][:, a * CAP:(a + 1) * CAP], w[:, c, m * P:(m + 1) * P],
                                                        XE[odd][:, c, :], start=(c == 0), stop=(c == KC - 1))
                        last.then_inc(gu_filled.sem, 1)
                    turn_rows(t.next())
                    pe.wait_ge(gu_ready.sem, t.value(gu_ready))
                    for k in range(ST):
                        pe.wait_ge(sum_ready.sem, t.value(sum_ready, k, back=1))
                        for m in range(FC):
                            last = nc.tensor.matmul(bank[DOWN[k]][:, :], HT[:, m, k * P:(k + 1) * P], WDn[odd][:, m, :],
                                                    start=(m == 0), stop=(m == FC - 1))
                        last.then_inc(dn_filled.sem, 1)

        @block.vector
        def _(dve):
            v = nc.vector
            wg_ready = sem("wg_ready")
            v.memset(tokens[:, ST * E:], NOWHERE)
            v.memset(OG[:, :, :], 0.0)
            v.memset(XG[1][:, :, :], 0.0)
            v.memset(XG[0][:, :, :], 0.0).then_inc(cleared, 1)
            def take_weights(t):
                dve.wait_ge(gathered[t.buf], t.pair * (16 * ST) + 16 * ST * (t.odd // 2 + 1))
                v.tensor_copy(WC[t.buf][:, :], XG[t.buf][:, :, bass.ds(t.pair * 2 + (DIM + t.odd), 1)]
                              .rearrange("p k o -> p (k o)")).then_inc(wc_ready.sem, 1)
                dve.wait_ge(wc_ready.sem, t.value(wc_ready))

            take_weights(Turn(0, 0))
            with dve.Fori(0, E // 2) as pair:
                for odd in range(2):
                    t = Turn(pair, odd)
                    for m in range(FC):
                        dve.wait_ge(gu_tanh.sem, t.value(gu_tanh, m))
                        b = bank[HID[m]]
                        v.scalar_tensor_tensor(WG[:, :], TG[:, :], 1.0, b[:, 0:CAP], ALU.add, ALU.mult).then_inc(wg_ready, 1)
                        dve.wait_ge(wg_ready, pair * 6 + (3 * odd + m + 1))
                        if m == 0:
                            dve.wait_ge(dn_filled.sem, t.value(dn_filled, back=1))
                        v.scalar_tensor_tensor(HT[:, m, :], WG[:, :], 0.5, b[:, CAP:2 * CAP], ALU.mult,
                                               ALU.mult).then_inc(gu_ready.sem, 1)
                        dve.wait_ge(gu_ready.sem, t.value(gu_ready, m))
                    take_weights(t.next())
                    dve.wait_ge(sums_in.sem, t.value(sums_in))
                    for k in range(ST):
                        dve.wait_ge(dn_filled.sem, t.value(dn_filled, k))
                        v.scalar_tensor_tensor(OG[:, k, :], bank[DOWN[k]][:, :], WC[odd][:, k:k + 1], OG[:, k, :], ALU.mult,
                                               ALU.add).then_inc(sum_ready.sem, 1)


_INS = ['L0_attn_x', 'L0_attn_Wq', 'L0_attn_bq', 'L0_attn_Wk', 'L0_attn_bk', 'L0_attn_Wv', 'L0_attn_bv',
        'L0_attn_Wg1', 'L0_attn_bg1', 'L0_attn_Wg2', 'L0_attn_bg2', 'L0_ffn_router_w', 'L0_ffn_w_gate',
        'L0_ffn_w_up', 'L0_ffn_w_down', 'L0_ffn_ws_gate_up', 'L0_ffn_ws_down']


def kernel(**inputs):
    import numpy as _np
    import concourse.bacc as _bacc
    from concourse import mybir as _mybir
    from concourse.bass_utils import run_bass_kernel_spmd as _run

    nc = _bacc.Bacc("TRN2", target_bir_lowering=False, num_devices=1)
    arrays, args = {}, []
    for name in _INS:
        a = _np.ascontiguousarray(inputs[name])
        arrays[f"in_{name}_dram"] = a
        args.append(nc.dram_tensor(f"in_{name}_dram", a.shape, _mybir.dt.from_np(a.dtype), kind="ExternalInput").ap())
    out = nc.dram_tensor("out_0_dram", (BATCH, LEN, DIM), _mybir.dt.float32, kind="ExternalOutput").ap()
    layer_kernel(nc, *args, out)
    r = _run(nc, [arrays], core_ids=[0])
    return r.results[0]["out_0_dram"]
```

```python
import math
from contextlib import ExitStack

import concourse.bass as bass
from concourse import mybir

ACT = mybir.ActivationFunctionType
ALU = mybir.AluOpType
AX = mybir.AxisListType
f32, f32r, bf16, i32 = mybir.dt.float32, mybir.dt.float32r, mybir.dt.bfloat16, mybir.dt.int32

P = 128
DIM = 512
KC = DIM // P
H, D = 16, 32
C = 64
HC = C // 2
GH = 16
GP = 128
BATCH, LEN = 2, 8192
NTOK = BATCH * LEN
TB = 256
NT = TB // P
NCH = TB // C
NBLK = NTOK // TB
E, TOPK, CAP = 64, 8, 256
F = 384
FC = F // P
SLOTS = E * CAP
ST = CAP // P
ROW = DIM + E
EPS = 1e-5
SCALE = 1.0 / math.sqrt(D)
NEG = -3.0e38
NOWHERE = 32768
GB = 4

WPART = KC * F
WCOLS = 3 * WPART
PIECES = ([slice(i * WPART // 2, (i + 1) * WPART // 2) for i in range(4)]
          + [slice(2 * WPART + i * DIM, 2 * WPART + (i + 1) * DIM) for i in range(FC)])

BANK_OF = {"G1": 0, "Qa": 1, "G2a": 2, "Qb": 3, "G2b": 0, "Ka": 1, "Kb": 2, "ATr0": 3, "V0": 0, "V1": 1, "ATr1": 2,
           "X2Ta": 3, "X2Tb": 0, "RL": 1, "GU0": 2, "RLT": 3, "GU1": 0, "GU2": 1, "KTok0": 2, "KTok1": 0, "DK": 3,
           "DN0": 1, "DN1": 2}
JOBS = list(BANK_OF)
PROJECT = ["G1", "Qa", "G2a", "Qb", "G2b", "Ka", "Kb", "V0", "V1", "KTok0", "KTok1", "DK"]


class Event:

    def __init__(self, sem, n, early):
        self.sem, self.n, self.early = sem, n, early

    def after(self, block, k):
        return self.early + self.n * block + k + 1


class Turn:

    def __init__(self, pair, odd):
        self.pair, self.odd = pair, odd

    def value(self, event, k=None, back=0):
        k = event.n - 1 if k is None else k
        return self.pair * (2 * event.n) + event.after(self.odd - back, k)

    def next(self, n=1):
        return Turn(self.pair, self.odd + n)

    @property
    def buf(self):
        return self.odd % 2


def layer_kernel(nc, x, Wq, bq, Wk, bk, Wv, bv, Wg1, bg1, Wg2, bg2, router_w, w_gate, w_up, w_down,
                 ws_gate_up, ws_down, out):
    x_rows = x.rearrange("b l d -> (b l) d").rearrange("(n t p) d -> n p t d", t=NT, p=P)
    out_flat = out.rearrange("b l d -> (b l) d")
    out_rows = out_flat.rearrange("(n t p) d -> n p t d", t=NT, p=P)
    norm_dram = nc.dram_tensor("norm_rows", (NTOK, ROW), f32, kind="Internal").ap()
    norm_rows = norm_dram.rearrange("(n t p) d -> n p t d", t=NT, p=P)
    table_dram = nc.dram_tensor("slot_tokens", (SLOTS, 1), i32, kind="Internal").ap()
    with nc.allow_non_contiguous_dma(reason="small weights and per-row pieces"):
        phase_tokens(nc, x_rows, Wq, bq, Wk, bk, Wv, bv, Wg1, bg1, Wg2, bg2, router_w,
                     ws_gate_up, ws_down, out_rows, norm_rows, table_dram)
        phase_experts(nc, w_gate, w_up, w_down, out_flat, norm_dram, table_dram)


def apart(engine, done):
    engine.sem_inc(done, 1)


def phase_tokens(nc, x_rows, Wq, bq, Wk, bk, Wv, bv, Wg1, bg1, Wg2, bg2, router_w, ws_gate_up,
                 ws_down, out_rows, norm_rows, table_dram):
    ctx = ExitStack()
    with ctx:
        def sb(name, shape, dt=f32):
            return ctx.enter_context(nc.sbuf_tensor(name, shape, dt))

        def sem(name):
            return ctx.enter_context(nc.semaphore(name))

        ident = sb("ident", [P, P])
        causal = sb("causal", [P, C])
        decay_mask = sb("decay_mask", [P, P])
        seg_start = sb("seg_start", [P, TB])
        before = sb("before", [P, P], bf16)
        ones_b = sb("ones_b", [P, P], bf16)
        slot_base = sb("slot_base", [P, E])
        neg_half = sb("neg_half", [P, NT])
        keep = sb("keep", [P, NBLK + 1])
        wq, wk, wv = ([sb(f"{n}{i}", [P, KC, DIM], f32r) for i in "hl"] for n in ("wq", "wk", "wv"))
        wsgu = [sb(f"wsgu{i}", [P, KC, 2 * F], f32r) for i in "hl"]
        wsd = [sb(f"wsd{i}", [P, FC, DIM], f32r) for i in "hl"]
        wg1 = [sb(f"wg1{i}", [P, KC, GP], f32r) for i in "hl"]
        wg2 = sb("wg2", [GP, DIM])
        rwT = [sb(f"rwT{i}", [P, KC, E], f32r) for i in "hl"]
        bq4 = sb("bq4", [P, KC])
        bk4 = sb("bk4", [P, KC])
        bvb = sb("bvb", [P, DIM])
        b1 = sb("b1", [GP, 1])
        b1h = sb("b1h", [GP, 1])
        b2 = sb("b2", [P, KC])
        b2h = sb("b2h", [P, KC])
        nowhere = sb("nowhere", [P, SLOTS // P], i32)
        X = [sb(f"X{i}", [P, NT, DIM]) for i in range(2)]
        st1 = sb("st1", [P, NT, 6])
        mv1 = sb("mv1", [P, NT, 2])
        ve1 = sb("ve1", [P, NT])
        rs1 = sb("rs1", [P, NT])
        sh1 = sb("sh1", [P, NT])
        XN = sb("XN", [P, NT, DIM])
        XT = [sb(f"XT{i}", [P, KC, TB], f32r) for i in "hl"]
        z1 = sb("z1", [GP, TB])
        t1 = sb("t1", [GP, TB])
        s1 = sb("s1", [GP, TB])
        AL = sb("AL", [P, KC, TB])
        EX = sb("EX", [P, KC, TB])
        QT = [sb(f"QT{i}", [P, KC, TB]) for i in range(2)]
        KT = [sb(f"KT{i}", [P, KC, TB]) for i in range(2)]
        QD = sb("QD", [P, KC, TB])
        KD = sb("KD", [P, KC, TB])
        FS = [sb(f"FS{i}", [P, KC, NCH, 2]) for i in range(2)]
        V = sb("V", [P, NT, DIM])
        V2 = sb("V2", [P, NT, DIM])
        KTok = sb("KTok", [P, NT, DIM])
        S = sb("S", [P, KC, D])
        U = sb("U", [P, KC, D])
        R = sb("R", [P, NCH, KC, D])
        MX = sb("MX", [P, 8])
        PR = [sb(f"PR{i}", [P, 8, C]) for i in range(2)]
        SU = sb("SU", [P, 8])
        RU = sb("RU", [P, 8])
        AM = [sb(f"AM{i}", [P, 4, P]) for i in range(2)]
        WT = [sb(f"WT{i}", [P, 4, P]) for i in range(2)]
        OTs = [sb(f"OTs{i}", [P, KC, P]) for i in range(2)]
        X2 = sb("X2", [P, NT, DIM])
        st2 = sb("st2", [P, NT, 6])
        mv2 = sb("mv2", [P, NT, 2])
        ve2 = sb("ve2", [P, NT])
        rs2 = sb("rs2", [P, NT])
        XR = sb("XR", [P, NT, ROW])
        LT = sb("LT", [E, TB])
        LG = sb("LG", [P, NT, E])
        rmx = sb("rmx", [P, NT])
        PB = sb("PB", [P, NT, E])
        rsu = sb("rsu", [P, NT])
        rre = sb("rre", [P, NT])
        top = sb("top", [P, NT, 8])
        RP = sb("RP", [P, NT, E])
        M = sb("M", [P, NT, E], bf16)
        PW = sb("PW", [P, NT, E])
        PO = sb("PO", [P, NT, E])
        VA = sb("VA", [P, NT, E])
        T1 = sb("T1", [P, NT, E])
        T2 = sb("T2", [P, NT, E])
        carry = sb("carry", [P, E])
        key8 = sb("key8", [P, NT, 8])
        slot8 = sb("slot8", [P, NT, 8], i32)
        tokf = sb("tokf", [P, NT])
        toki = sb("toki", [P, NT], i32)
        TG = sb("TG", [P, TB])
        WG = sb("WG", [P, TB])
        HT = [sb(f"HT{i}", [P, FC, TB], f32r) for i in "hl"]

        bank = [ctx.enter_context(nc.psum_tensor(f"bank{i}", [P, 512], f32)) for i in range(GB)]
        s_bank = ctx.enter_context(nc.psum_tensor("s_bank", [P, 512], f32))
        pt_bank = ctx.enter_context(nc.psum_tensor("pt_bank", [P, 512], f32))
        a_bank = ctx.enter_context(nc.psum_tensor("a_bank", [P, 512], f32))
        ot_bank = ctx.enter_context(nc.psum_tensor("ot_bank", [P, 512], f32))

        begun = sem("begun")
        consts_made = sem("consts_made")
        consts_done = sem("consts_done")
        gate_clear = sem("gate_clear")
        weights_in = sem("weights_in")
        table_clear = sem("table_clear")
        rw_turned = sem("rw_turned")
        rw_ready = sem("rw_ready")
        w_high = sem("w_high")
        w_low = sem("w_low")
        pool_chain = sem("pool_chain")
        pe_apart, dve_apart, pool_apart, sp_apart = (sem(f"{e}_apart") for e in ("pe", "dve", "pool", "sp"))

        primed = []

        def event(name, n=1):
            primed.append(Event(sem(name), n, n))
            return primed[-1]

        x_loaded = event("x_loaded", 16)
        v_swapped = event("v_swapped", 32)
        rows_stored = event("rows_stored", 16)
        out_stored = event("out_stored", 16)
        scattered = Event(sem("scattered"), 16 * TOPK * NT, 0)
        slots_used = event("slots_used")
        var1_ready = event("var1_ready")
        rstd1_ready = event("rstd1_ready")
        shift1_ready = event("shift1_ready")
        xn_ready = event("xn_ready")
        xt_filled = event("xt_filled", 2)
        xh_ready = event("xh_ready", 2)
        xl_ready = event("xl_ready", 2)
        g1_filled = event("g1_filled")
        g1_tanh = event("g1_tanh", 2)
        s1_ready = event("s1_ready")
        g2_filled = event("g2_filled", 2)
        th_ready = event("th_ready", 4)
        al_ready = event("al_ready")
        q_filled = event("q_filled", 2)
        q_ready = event("q_ready", 4)
        k_filled = event("k_filled", 2)
        k_ready = event("k_ready", 4)
        fs_ready = event("fs_ready")
        inverted = event("inverted")
        qd_half = event("qd_half")
        kd_half = event("kd_half")
        qd_ready = event("qd_ready")
        kd_ready = event("kd_ready")
        v_filled = event("v_filled", 2)
        v_ready = event("v_ready", 2)
        ktok_filled = event("ktok_filled", 2)
        ktok_ready = event("ktok_ready", 2)
        dk_filled = event("dk_filled", 2)
        r_ready = event("r_ready", 4)
        dk_used = event("dk_used")
        s_rows = event("s_rows", 12)
        a_rows = event("a_rows", 12)
        s_filled = event("s_filled", 4)
        s_masked = event("s_masked", 4)
        a_filled = event("a_filled", 4)
        a_masked = event("a_masked", 4)
        shifted = event("shifted", 4)
        exped = event("exped", 4)
        p_ready = event("p_ready", 4)
        pt_filled = event("pt_filled", 4)
        w_ready = event("w_ready", 4)
        ot_filled = event("ot_filled", 4)
        ot_evac = event("ot_evac", 4)
        at_filled = event("at_filled", 2)
        x2_ready = event("x2_ready", 2)
        var2_ready = event("var2_ready", 2)
        rstd2_ready = event("rstd2_ready", 2)
        x2n_ready = event("x2n_ready", 2)
        x2t_filled = event("x2t_filled", 2)
        x2h_ready = event("x2h_ready", 2)
        x2l_ready = event("x2l_ready", 2)
        rl_filled = event("rl_filled")
        lt_ready = event("lt_ready")
        rlt_filled = event("rlt_filled")
        logits_shifted = event("logits_shifted")
        router_exped = event("router_exped")
        m_ready = event("m_ready")
        rows_ready = event("rows_ready")
        pos_filled = event("pos_filled")
        pos_used = event("pos_used")
        slots_ready = event("slots_ready")
        gu_filled = event("gu_filled", 3)
        gu_tanh = event("gu_tanh", 3)
        gu_ready = event("gu_ready", 3)
        hh_ready = event("hh_ready", 3)
        hl_ready = event("hl_ready", 3)
        dn_filled = event("dn_filled", 2)
        out_ready = event("out_ready", 2)
        dve_chain = sem("dve_chain")

        READ = {"DK": (dk_used, 0), "G1": (g1_tanh, 1),
                "Qa": (q_ready, 1), "Qb": (q_ready, 3), "G2a": (th_ready, 1), "G2b": (th_ready, 3),
                "Ka": (k_ready, 1), "Kb": (k_ready, 3), "ATr0": (x2_ready, 0), "ATr1": (x2_ready, 1),
                "V0": (v_ready, 0), "V1": (v_ready, 1), "KTok0": (ktok_ready, 0), "KTok1": (ktok_ready, 1),
                "X2Ta": (x2l_ready, 0), "X2Tb": (x2l_ready, 1), "RL": (lt_ready, 0),
                "RLT": (logits_shifted, 0), "GU0": (gu_ready, 0),
                "GU1": (gu_ready, 1), "GU2": (gu_ready, 2), "DN0": (out_ready, 0), "DN1": (out_ready, 1)}

        XT_BANK = (s_bank, pt_bank)

        POS_COLS = slice(2 * P, 2 * P + 3 * E)

        def bank_of(job):
            return bank[BANK_OF[job]]

        def pieces_of(w, chunks, width):
            return [w[:, 0:chunks, i:i + TB] for i in range(0, width, TB)]

        stages = [QT[0], QT[1], KT[0], KT[1], QD, KD, V, V2, KTok, AL, EX]
        staged = []
        for w, src, chunks, width in ((wq, Wq, KC, DIM), (wk, Wk, KC, DIM), (wv, Wv, KC, DIM),
                                      (wsgu, ws_gate_up, KC, 2 * F), (wsd, ws_down, FC, DIM)):
            rows = src.rearrange("(c p) n -> p c n", p=P)
            for i, (high, low) in enumerate(zip(pieces_of(w[0], chunks, width), pieces_of(w[1], chunks, width))):
                st = stages[len(staged)]
                st = (st[:, :, :].rearrange("p a b -> p (a b)")[:, 0:chunks * TB].rearrange("p (c n) -> p c n", c=chunks))
                staged.append((st, high, low, rows[:, :, i * TB:(i + 1) * TB]))
        wg1_f = XR[:, 1, 0:KC * GP].rearrange("p (c n) -> p c n", c=KC)
        rw = XR[0:E, 0, 0:DIM]
        staged.append((wg1_f, wg1[0][:, :, :], wg1[1][:, :, :], None))
        WEIGHT_DMAS = 8
        piece_in = [sem(f"piece_in{i}") for i in range(len(staged) - 1)]

        def heads(half, r=None):
            return [(4 * g + q, g, q) for g in (2 * half, 2 * half + 1) for q in range(4) if r in (None, q)]

        block = ctx.enter_context(nc.Block())

        @block.sync
        def _(sp):
            def load_x(t):
                sp.dma_start(X[t.buf][:, :, :], x_rows[t.pair * 2 + t.odd, :, :, :]).then_inc(x_loaded.sem, 16)

            sp.wait_ge(begun, 1)
            load_x(Turn(0, 0))
            for (dst, _, _, src), come in zip(staged[:-1], piece_in):
                sp.dma_start(dst, src).then_inc(come, 16)
            sp.wait_ge(gate_clear, 1)
            sp.dma_start(wg1_f[:, :, 0:GH], Wg1.rearrange("(c p) n -> p c n", p=P)).then_inc(weights_in, 16)
            sp.dma_start(wg2[0:GH, :], Wg2).then_inc(weights_in, 16)
            sp.dma_start(rw, router_w).then_inc(weights_in, 16)
            for dst, src in ((bq4, bq), (bk4, bk), (b2, bg2)):
                sp.dma_start(dst[:, :], src.rearrange("(c p) -> p c", p=P)).then_inc(weights_in, 16)
            sp.dma_start(b1[0:GH, :], bg1.rearrange("(p o) -> p o", o=1)).then_inc(weights_in, 16)
            sp.dma_start(bvb[:, :], bv.rearrange("(o n) -> o n", o=1).to_broadcast([P, DIM])).then_inc(weights_in, 16)
            load_x(Turn(0, 1))

            def swap_v(t):
                sp.wait_ge(ot_filled.sem, t.value(ot_filled, back=1))
                apart(sp, sp_apart)
                sp.wait_ge(v_ready.sem, t.value(v_ready))
                for a, b in ((0, C), (C, 0)):
                    sp.dma_start(V2[a:a + C, :, :], V[b:b + C, :, :]).then_inc(v_swapped.sem, 16)

            swap_v(Turn(0, 0))
            sp.wait_ge(consts_made, 1)
            sp.dma_start(table_dram.rearrange("(p c) o -> p (c o)", p=P), nowhere[:, :]).then_inc(table_clear, 16)

            def turn(t, last):
                sp.wait_ge(x2_ready.sem, t.value(x2_ready))
                if last:
                    sp.dma_start(X[t.buf][:, :, :], x_rows[0, :, :, :]).then_inc(x_loaded.sem, 16)
                else:
                    load_x(Turn(t.pair, t.odd + 2))
                swap_v(t.next())
                sp.wait_ge(rows_ready.sem, t.value(rows_ready))
                sp.dma_start(norm_rows[t.pair * 2 + t.odd, :, :, :], XR[:, :, :]).then_inc(rows_stored.sem, 16)
                sp.wait_ge(out_ready.sem, t.value(out_ready))
                sp.dma_start(out_rows[t.pair * 2 + t.odd, :, :, :], X2[:, :, :]).then_inc(out_stored.sem, 16)

            with sp.Fori(0, NBLK // 2 - 1) as pair:
                for odd in range(2):
                    turn(Turn(pair, odd), False)
            end = NBLK // 2 - 1
            for odd in range(2):
                turn(Turn(end, odd), True)
            sp.wait_ge(x_loaded.sem, 16 * (NBLK + 3))
            sp.wait_ge(v_swapped.sem, 32 * (NBLK + 2))
            sp.wait_ge(rows_stored.sem, 16 * (NBLK + 1))
            sp.wait_ge(out_stored.sem, 16 * (NBLK + 1))

        @block.gpsimd
        def _(pool):
            links = [0]

            def link(ins):
                links[0] += 1
                ins.then_inc(pool_chain, 1)
                pool.wait_ge(pool_chain, links[0])

            for ev in primed:
                pool.sem_inc(ev.sem, ev.early)
            pool.sem_inc(begun, 1)
            nc.gpsimd.memset(wg1_f, 0.0)
            nc.gpsimd.memset(wg2[:, :], 0.0)
            nc.gpsimd.memset(b1[:, :], 0.0).then_inc(gate_clear, 1)
            link(nc.gpsimd.memset(nowhere[:, :], NOWHERE))
            link(nc.gpsimd.memset(ident[:, :], 0.0))
            link(nc.gpsimd.affine_select(out=ident[:, :], in_=ident[:, :], compare_op=ALU.not_equal, fill=1.0,
                                         base=0, pattern=[[-1, P]], channel_multiplier=1))
            link(nc.gpsimd.memset(causal[:, :], 0.0))
            for h in range(2):
                link(nc.gpsimd.affine_select(out=causal[h * C:(h + 1) * C, :], in_=causal[h * C:(h + 1) * C, :],
                                             compare_op=ALU.is_ge, fill=NEG, base=0, pattern=[[-1, C]],
                                             channel_multiplier=1))
            link(nc.gpsimd.memset(decay_mask[:, :], 1.0))
            for h in range(2):
                link(nc.gpsimd.affine_select(out=decay_mask[h * C:(h + 1) * C, :],
                                             in_=decay_mask[h * C:(h + 1) * C, :], compare_op=ALU.is_gt,
                                             fill=0.0, base=0, pattern=[[0, 2], [1, C]], channel_multiplier=-1))
            link(nc.gpsimd.memset(before[:, :], 1.0))
            link(nc.gpsimd.affine_select(out=before[:, :], in_=before[:, :], compare_op=ALU.is_gt, fill=0.0,
                                         base=0, pattern=[[1, P]], channel_multiplier=-1))
            link(nc.gpsimd.memset(ones_b[:, :], 1.0))
            link(nc.gpsimd.iota(slot_base[:, :], pattern=[[2, E]], base=0, channel_multiplier=0,
                                allow_small_or_imprecise_dtypes=True))
            link(nc.gpsimd.iota(tokf[:, :], pattern=[[P, NT]], base=0, channel_multiplier=1,
                                allow_small_or_imprecise_dtypes=True))
            link(nc.gpsimd.memset(seg_start[:, :], 0.0))
            link(nc.gpsimd.memset(seg_start[:, :].rearrange("p (s t) -> p s t", t=HC)[:, :, 0:1], 1.0))
            link(nc.gpsimd.memset(keep[:, :], 1.0))
            link(nc.gpsimd.memset(keep[:, 0:NBLK:NBLK // BATCH], 0.0))
            nc.gpsimd.memset(neg_half[:, :], -0.5).then_inc(consts_made, 1)
            pool.wait_ge(consts_made, 1)

            def rstd1(t):
                pool.wait_ge(var1_ready.sem, t.value(var1_ready))
                nc.gpsimd.tensor_tensor(rs1[:, :], ve1[:, :], neg_half[:, :], ALU.pow).then_inc(rstd1_ready.sem, 1)

            def rstd2(t, k):
                pool.wait_ge(var2_ready.sem, t.value(var2_ready, k))
                nc.gpsimd.tensor_tensor(rs2[:, k:k + 1], ve2[:, k:k + 1], neg_half[:, k:k + 1],
                                        ALU.pow).then_inc(rstd2_ready.sem, 1)

            def bc(ap, n):
                return ap.unsqueeze(2).to_broadcast([ap.shape[0], ap.shape[1], n])

            def decayed_q(t):
                pool.wait_ge(q_ready.sem, t.value(q_ready))
                pool.wait_ge(inverted.sem, t.value(inverted))
                pool.wait_ge(ot_filled.sem, t.value(ot_filled, back=1))
                apart(pool, pool_apart)
                nc.gpsimd.tensor_tensor(QD[:, :, :], QT[t.buf][:, :, :], EX[:, :, :], ALU.mult).then_inc(qd_half.sem, 1)
                pool.wait_ge(qd_half.sem, t.value(qd_half))
                apart(pool, pool_apart)
                first = QD[:, :, :].rearrange("p c (n s) -> p (c n) s", s=C)[:, :, 0:HC]
                r = AL[:, :, :].rearrange("p c (n s) -> p (c n) s", s=C)[:, :, HC - 1]
                nc.gpsimd.tensor_tensor(first, first, bc(r, HC), ALU.mult).then_inc(qd_ready.sem, 1)

            def decayed_k(t):
                pool.wait_ge(k_ready.sem, t.value(k_ready))
                pool.wait_ge(inverted.sem, t.value(inverted))
                pool.wait_ge(a_filled.sem, t.value(a_filled, back=1))
                pool.wait_ge(ktok_filled.sem, t.value(ktok_filled, back=1))
                apart(pool, pool_apart)
                nc.gpsimd.tensor_tensor(KD[:, :, :], KT[t.buf][:, :, :], AL[:, :, :], ALU.mult).then_inc(kd_half.sem, 1)
                pool.wait_ge(kd_half.sem, t.value(kd_half))
                apart(pool, pool_apart)
                first = KD[:, :, :].rearrange("p c (n s) -> p (c n) s", s=C)[:, :, 0:HC]
                m = FS[t.buf][:, :, :, 0].rearrange("p c n -> p (c n)")
                nc.gpsimd.tensor_tensor(first, first, bc(m, HC), ALU.mult).then_inc(kd_ready.sem, 1)

            def scatter(t):
                pool.wait_ge(slots_ready.sem, t.value(slots_ready))
                apart(pool, pool_apart)
                for tile in range(NT):
                    for k in range(TOPK):
                        nc.gpsimd.indirect_dma_start(
                            out=table_dram, out_offset=bass.IndirectOffsetOnAxis(ap=slot8[:, tile, k:k + 1], axis=0),
                            in_=toki[:, tile:tile + 1], in_offset=None, bounds_check=SLOTS - 1,
                            oob_is_err=False).then_inc(scattered.sem, 16)
                pool.wait_ge(scattered.sem, t.value(scattered))
                pool.sem_inc(slots_used.sem, 1)

            rstd1(Turn(0, 0))
            decayed_q(Turn(0, 0))
            decayed_k(Turn(0, 0))
            rstd1(Turn(0, 1))
            pool.wait_ge(table_clear, 16)
            with pool.Fori(0, NBLK // 2) as pair:
                for odd in range(2):
                    t = Turn(pair, odd)
                    for k in range(NT):
                        rstd2(t, k)
                    rstd1(t.next(2))
                    decayed_k(t.next())
                    decayed_q(t.next())
                    scatter(t)

        @block.scalar
        def _(act):
            def normalise(t):
                act.wait_ge(shift1_ready.sem, t.value(shift1_ready))
                act.wait_ge(xt_filled.sem, t.value(xt_filled, back=1))
                for k in range(NT):
                    ins = nc.scalar.activation(XN[:, k, :], X[t.buf][:, k, :], ACT.Identity, bias=sh1[:, k:k + 1],
                                               scale=rs1[:, k:k + 1])
                ins.then_inc(xn_ready.sem, 1)

            def xt_evac(t):
                act.wait_ge(gu_filled.sem, t.value(gu_filled, back=2))
                for k in range(2):
                    act.wait_ge(xt_filled.sem, t.value(xt_filled, k))
                    nc.scalar.activation(XT[0][:, 2 * k:2 * k + 2, :], XT_BANK[k][:, :].rearrange("p (a b) -> p a b", a=2),
                                         ACT.Copy).then_inc(xh_ready.sem, 1)

            def gate1(t):
                act.wait_ge(g1_filled.sem, t.value(g1_filled))
                act.wait_ge(s1_ready.sem, t.value(s1_ready, back=1))
                nc.scalar.activation(t1[:, :], bank_of("G1")[0:GP, 0:TB], ACT.Tanh, bias=b1h[:, :], scale=0.5).then_inc(g1_tanh.sem, 1)
                nc.scalar.activation(z1[:, :], bank_of("G1")[0:GP, 0:TB], ACT.Identity, bias=b1[:, :], scale=1.0).then_inc(g1_tanh.sem, 1)

            def gate2(t, k):
                act.wait_ge(g2_filled.sem, t.value(g2_filled, k))
                if k == 0:
                    act.wait_ge(kd_ready.sem, t.value(kd_ready, back=1))
                for m in (2 * k, 2 * k + 1):
                    nc.scalar.activation(AL[:, m, :], bank_of("G2a" if k == 0 else "G2b")[:, (m % 2) * TB:(m % 2 + 1) * TB],
                                         ACT.Tanh, bias=b2h[:, m:m + 1], scale=0.25).then_inc(th_ready.sem, 1)

            def alpha(t):
                act.wait_ge(th_ready.sem, t.value(th_ready))
                nc.scalar.activation(AL[:, :, :], AL[:, :, :], ACT.Copy, bias=0.55, scale=0.45).then_inc(al_ready.sem, 1)

            def qk_evac(t, k, filled, ready, dst, bias, names):
                act.wait_ge(filled.sem, t.value(filled, k))
                for m in (2 * k, 2 * k + 1):
                    nc.scalar.activation(dst[t.buf][:, m, :], bank_of(names[k])[:, (m % 2) * TB:(m % 2 + 1) * TB],
                                         ACT.Identity, bias=bias[:, m:m + 1], scale=1.0).then_inc(ready.sem, 1)

            def ktok_evac(t, k):
                act.wait_ge(ktok_filled.sem, t.value(ktok_filled, k))
                act.wait_ge(dk_filled.sem, t.value(dk_filled, back=1))
                nc.scalar.activation(KTok[:, k, :], bank_of(f"KTok{k}")[:, :], ACT.Copy).then_inc(ktok_ready.sem, 1)

            def exp(t, u):
                act.wait_ge(shifted.sem, t.value(shifted, u))
                nc.scalar.activation(PR[u % 2][:, :, :], PR[u % 2][:, :, :], ACT.Exp, scale=SCALE).then_inc(exped.sem, 1)

            def ot(t, u):
                act.wait_ge(ot_filled.sem, t.value(ot_filled, u))
                if u % 2 == 0:
                    act.wait_ge(at_filled.sem, t.value(at_filled, back=1))
                nc.scalar.activation(OTs[u // 2][:, 2 * (u % 2):2 * (u % 2) + 2, :],
                                     ot_bank[:, 0:2 * P].rearrange("p (a b) -> p a b", a=2),
                                     ACT.Copy).then_inc(ot_evac.sem, 1)

            def x2t(t):
                act.wait_ge(v_filled.sem, t.next().value(v_filled))
                for k in range(2):
                    act.wait_ge(x2t_filled.sem, t.value(x2t_filled, k))
                    nc.scalar.activation(XT[0][:, 2 * k:2 * k + 2, :], bank_of("X2Ta" if k == 0 else "X2Tb")[:, :]
                                         .rearrange("p (a b) -> p a b", a=2), ACT.Copy).then_inc(x2h_ready.sem, 1)

            def hidden_high(t, m):
                act.wait_ge(gu_ready.sem, t.value(gu_ready, m))
                if m == 0:
                    act.wait_ge(dn_filled.sem, t.value(dn_filled, back=1))
                nc.scalar.activation(HT[0][:, m, :], WG[:, :], ACT.Copy).then_inc(hh_ready.sem, 1)

            def lt(t):
                act.wait_ge(rl_filled.sem, t.value(rl_filled))
                act.wait_ge(rlt_filled.sem, t.value(rlt_filled, back=1))
                nc.scalar.activation(LT[:, :], bank_of("RL")[0:E, 0:TB], ACT.Copy).then_inc(lt_ready.sem, 1)

            def router_exp(t):
                act.wait_ge(logits_shifted.sem, t.value(logits_shifted))
                nc.scalar.activation(PB[:, :, :], LG[:, :, :], ACT.Exp).then_inc(router_exped.sem, 1)

            def gu(t, m):
                act.wait_ge(gu_filled.sem, t.value(gu_filled, m))
                if m == 0:
                    act.wait_ge(gu_ready.sem, t.value(gu_ready, back=1))
                else:
                    act.wait_ge(gu_ready.sem, t.value(gu_ready, m - 1))
                nc.scalar.activation(TG[:, :], bank_of(f"GU{m}")[:, 0:TB], ACT.Tanh, scale=0.5).then_inc(gu_tanh.sem, 1)

            for i, (piece, high, _, _) in enumerate(staged):
                if i < len(piece_in):
                    act.wait_ge(piece_in[i], 16)
                else:
                    act.wait_ge(weights_in, 16 * WEIGHT_DMAS)
                    act.wait_ge(rw_turned, 1)
                nc.scalar.activation(high, piece, ACT.Copy).then_inc(w_high, 1)
            nc.scalar.activation(rwT[0][:, :, :], bank[0][:, 0:KC * E].rearrange("p (a b) -> p a b", a=KC), ACT.Copy).then_inc(rw_ready, 1)
            nc.scalar.mul(b1h[:, :], b1[:, :], 0.5).then_inc(rw_ready, 1)
            nc.scalar.mul(b2h[:, :], b2[:, :], 0.5).then_inc(rw_ready, 1)
            act.wait_ge(rw_ready, 3)

            def q_evac(t, k):
                qk_evac(t, k, q_filled, q_ready, QT, bq4, ("Qa", "Qb"))

            def k_evac(t, k):
                qk_evac(t, k, k_filled, k_ready, KT, bk4, ("Ka", "Kb"))

            act.wait_ge(w_low, len(staged) + 1)
            t = Turn(0, 0)
            normalise(t)
            xt_evac(t)
            gate1(t)
            q_evac(t, 0)
            for k in range(2):
                gate2(t, k)
            alpha(t)
            q_evac(t, 1)
            for k in range(2):
                k_evac(t, k)
            for k in range(2):
                ktok_evac(t, k)
            act.wait_ge(v_filled.sem, t.value(v_filled))
            normalise(t.next())
            xt_evac(t.next())
            with act.Fori(0, NBLK // 2) as pair:
                for odd in range(2):
                    t = Turn(pair, odd)
                    n = t.next()
                    exp(t, 0)
                    gate1(n)
                    q_evac(n, 0)
                    exp(t, 1)
                    gate2(n, 0)
                    gate2(n, 1)
                    alpha(n)
                    ot(t, 0)
                    k_evac(n, 0)
                    exp(t, 2)
                    q_evac(n, 1)
                    ot(t, 1)
                    exp(t, 3)
                    k_evac(n, 1)
                    ot(t, 2)
                    ot(t, 3)
                    x2t(t)
                    lt(t)
                    gu(t, 0)
                    hidden_high(t, 0)
                    router_exp(t)
                    gu(t, 1)
                    hidden_high(t, 1)
                    normalise(t.next(2))
                    gu(t, 2)
                    ktok_evac(n, 0)
                    hidden_high(t, 2)
                    ktok_evac(n, 1)
                    xt_evac(t.next(2))

        @block.tensor
        def _(pe):
            seen = []

            def take(job, t, jobs):
                at = jobs.index(job)
                mine = BANK_OF[job]
                prior = [j for j in jobs[:at] if BANK_OF[j] == mine]
                back = 0
                if not prior:
                    if jobs is PROJECT:
                        return bank_of(job)
                    prior = [j for j in jobs if BANK_OF[j] == mine]
                    back = 1
                name = prior[-1]
                ev, k = READ[name]
                owner = t if (name not in PROJECT or jobs is PROJECT) else t.next()
                pe.wait_ge(ev.sem, owner.value(ev, k, back=back))
                return bank_of(job)

            def split_product(out, stationary, moving, first=True, last=True):
                (sh, sl), (mh, ml) = stationary, moving
                nc.tensor.matmul(out, sh, mh, start=first, stop=False)
                nc.tensor.matmul(out, sh, ml, start=False, stop=False)
                return nc.tensor.matmul(out, sl, mh, start=False, stop=last)

            def both(pair, *at):
                return [p[at] for p in pair]

            ALL = slice(None)

            def xt(t, k):
                b = XT_BANK[k]
                pe.wait_ge(xn_ready.sem, t.value(xn_ready))
                for a in range(2):
                    for tile in range(NT):
                        last = nc.tensor.transpose(b[:, a * TB + tile * P:a * TB + (tile + 1) * P],
                                                   XN[:, tile, (2 * k + a) * P:(2 * k + a + 1) * P], ident[:, :])
                last.then_inc(xt_filled.sem, 1)

            def gate1(t, jobs=JOBS):
                b = take("G1", t, jobs)
                o = t if jobs is PROJECT else t.next()
                pe.wait_ge(xl_ready.sem, o.value(xl_ready))
                for c in range(KC):
                    last = split_product(b[0:GP, 0:TB], both(wg1, ALL, c, ALL), both(XT, ALL, c, ALL), c == 0, c == KC - 1)
                last.then_inc(g1_filled.sem, 1)

            def gate2(t, k, jobs=JOBS):
                b = take("G2a" if k == 0 else "G2b", t, jobs)
                o = t if jobs is PROJECT else t.next()
                pe.wait_ge(s1_ready.sem, o.value(s1_ready))
                for a in range(2):
                    m = 2 * k + a
                    last = nc.tensor.matmul(b[:, a * TB:(a + 1) * TB], wg2[:, m * P:(m + 1) * P], s1[:, :], start=True, stop=True)
                last.then_inc(g2_filled.sem, 1)

            def project(t, k, w, filled, names, jobs=JOBS, parts=(0, 1)):
                b = take(names[k], t, jobs) if 0 in parts else bank_of(names[k])
                for a in parts:
                    m = 2 * k + a
                    for c in range(KC):
                        last = split_product(b[:, a * TB:(a + 1) * TB], both(w, ALL, c, slice(m * P, (m + 1) * P)),
                                             both(XT, ALL, c, ALL), c == 0, c == KC - 1)
                if 1 in parts:
                    last.then_inc(filled.sem, 1)

            def values(t, tile, jobs=JOBS, chunks=range(KC)):
                b = take(f"V{tile}", t, jobs) if 0 in chunks else bank_of(f"V{tile}")
                for c in chunks:
                    last = split_product(b[:, :], both(XT, ALL, c, slice(tile * P, (tile + 1) * P)), both(wv, ALL, c, ALL),
                                         c == 0, c == KC - 1)
                if KC - 1 in chunks:
                    last.then_inc(v_filled.sem, 1)

            def ktok(t, tile, jobs=JOBS):
                b = take(f"KTok{tile}", t, jobs)
                o = t if jobs is PROJECT else t.next()
                pe.wait_ge(kd_ready.sem, o.value(kd_ready))
                for g in range(KC):
                    last = nc.tensor.transpose(b[:, g * P:(g + 1) * P], KD[:, g, tile * P:(tile + 1) * P], ident[:, :])
                last.then_inc(ktok_filled.sem, 1)

            def state_updates(t, odd, jobs=JOBS):
                o = t if jobs is PROJECT else t.next()
                pe.wait_ge(ktok_ready.sem, o.value(ktok_ready))
                pe.wait_ge(v_ready.sem, o.value(v_ready))
                if odd == 0:
                    b = take("DK", t, jobs)
                else:
                    b = bank_of("DK")
                    pe.wait_ge(dk_filled.sem, o.value(dk_filled, 0))
                apart(pe, pe_apart)
                rows = slice(C * odd, C * odd + C)
                for c in range(odd, NCH, 2):
                    for h in range(H):
                        g, r = divmod(h, 4)
                        col = (c * KC + g) * D
                        last = nc.tensor.matmul(b[D * r:D * r + D, col:col + D],
                                                KTok[rows, c // 2, h * D:(h + 1) * D],
                                                V[rows, c // 2, h * D:(h + 1) * D], start=True, stop=True)
                last.then_inc(dk_filled.sem, 1)

            def scores(t, u, groups=range(4)):
                tile, half = divmod(u, 2)
                if u == 0 and 0 in groups:
                    pe.wait_ge(qd_ready.sem, t.value(qd_ready))
                    pe.wait_ge(kd_ready.sem, t.value(kd_ready))
                if 0 in groups:
                    pe.wait_ge(s_masked.sem, t.value(s_masked, u - 1))
                    pe.wait_ge(a_masked.sem, t.value(a_masked, u - 1))
                    if u == 0:
                        pe.wait_ge(xl_ready.sem, t.next().value(xl_ready, 0))
                q, k, qd, kd = QT[t.buf], KT[t.buf], QD, KD
                for r in groups:
                    rows = slice(D * r, D * r + D)
                    if r:
                        pe.wait_ge(s_rows.sem, t.value(s_rows, 3 * u + r - 1))
                    apart(pe, pe_apart)
                    for h, g, _ in heads(half, r):
                        n = h - 8 * half
                        for cc in range(2):
                            at = (2 * tile + cc) * C
                            last_s = nc.tensor.matmul(s_bank[C * cc:C * cc + C, n * C:n * C + C], q[rows, g, at:at + C],
                                                      k[rows, g, at:at + C], start=True, stop=True)
                    if r == 3:
                        last_s.then_inc(s_filled.sem, 1)
                    else:
                        last_s.then_inc(s_rows.sem, 1)
                    if r:
                        pe.wait_ge(a_rows.sem, t.value(a_rows, 3 * u + r - 1))
                        apart(pe, pe_apart)
                    for h, g, _ in heads(half, r):
                        n = h - 8 * half
                        for cc in range(2):
                            at = (2 * tile + cc) * C
                            for kh in range(2):
                                part = C * (n % 2) + HC * kh
                                col = (n // 2) * P + C * cc
                                last_a = nc.tensor.matmul(a_bank[part:part + HC, col + HC * kh:col + C],
                                                          kd[rows, g, at + HC * kh:at + HC * kh + HC],
                                                          qd[rows, g, at + HC * kh:at + C], start=True, stop=True)
                    last_a.then_inc(a_filled.sem if r == 3 else a_rows.sem, 1)

            def turn_probs(t, u):
                pe.wait_ge(p_ready.sem, t.value(p_ready, u))
                pe.wait_ge(w_ready.sem, t.value(w_ready, u - 1) if u else t.value(w_ready, back=1))
                if u == 0:
                    pe.wait_ge(xl_ready.sem, t.next().value(xl_ready, 1))
                for hp in range(4):
                    last = nc.tensor.transpose(pt_bank[:, hp * P:(hp + 1) * P],
                                               PR[u % 2][:, 2 * hp:2 * hp + 2, :].rearrange("p a b -> p (a b)"), ident[:, :])
                last.then_inc(pt_filled.sem, 1)

            def outputs(t, u):
                tile, half = divmod(u, 2)
                pe.wait_ge(w_ready.sem, t.value(w_ready, u))
                if u == 0:
                    pe.wait_ge(v_swapped.sem, t.value(v_swapped))
                if u % 2 == 0:
                    pe.wait_ge(r_ready.sem, t.value(r_ready, 2 * tile + 1))
                pe.wait_ge(ot_evac.sem, t.value(ot_evac, u - 1))
                if u == 0:
                    pe.wait_ge(pos_used.sem, t.value(pos_used, back=1))
                apart(pe, pe_apart)
                started = set()
                for h2 in range(2):
                    rows = slice(C * h2, C * h2 + C)
                    for h, g, r in heads(half):
                        if h % 2 != h2:
                            continue
                        for cc in range(2):
                            v = V if h2 == cc else V2
                            col = (g - 2 * half) * P + C * cc
                            nc.tensor.matmul(ot_bank[D * r:D * r + D, col:col + C], v[rows, tile, h * D:(h + 1) * D],
                                             WT[u % 2][rows, (h - 8 * half) // 2, C * cc:C * cc + C],
                                             start=r not in started, stop=False, skip_group_check=True)
                            started.add(r)
                for r in range(4):
                    for h, g, _ in heads(half, r):
                        for cc in range(2):
                            c = 2 * tile + cc
                            col = (g - 2 * half) * P + C * cc
                            last = nc.tensor.matmul(ot_bank[D * r:D * r + D, col:col + C], R[D * r:D * r + D, c, g, :],
                                                    QD[D * r:D * r + D, g, c * C:(c + 1) * C],
                                                    start=False, stop=True, skip_group_check=True)
                last.then_inc(ot_filled.sem, 1)

            def turn_out(t, tile):
                b = take(f"ATr{tile}", t, JOBS)
                pe.wait_ge(ot_evac.sem, t.value(ot_evac, 2 * tile + 1))
                for g in range(KC):
                    last = nc.tensor.transpose(b[:, g * P:(g + 1) * P], OTs[tile][:, g, :], ident[:, :])
                last.then_inc(at_filled.sem, 1)

            def x2t(t, tile):
                pe.wait_ge(x2n_ready.sem, t.value(x2n_ready, tile))
                for k in range(2):
                    name = "X2Ta" if k == 0 else "X2Tb"
                    b = take(name, t, JOBS) if tile == 0 else bank_of(name)
                    for a in range(2):
                        last = nc.tensor.transpose(b[:, a * TB + tile * P:a * TB + (tile + 1) * P],
                                                   XR[:, tile, (2 * k + a) * P:(2 * k + a + 1) * P], ident[:, :])
                    if tile == NT - 1:
                        last.then_inc(x2t_filled.sem, 1)

            def router(t):
                b = take("RL", t, JOBS)
                for c in range(KC):
                    if c % 2 == 0:
                        pe.wait_ge(x2l_ready.sem, t.value(x2l_ready, c // 2))
                    last = split_product(b[0:E, 0:TB], both(rwT, ALL, c, ALL), both(XT, ALL, c, ALL), c == 0, c == KC - 1)
                last.then_inc(rl_filled.sem, 1)

            def turn_logits(t):
                b = take("RLT", t, JOBS)
                pe.wait_ge(lt_ready.sem, t.value(lt_ready))
                apart(pe, pe_apart)
                for tile in range(NT):
                    last = nc.tensor.transpose(b[:, tile * E:(tile + 1) * E], LT[:, tile * P:(tile + 1) * P], ident[0:E, 0:E])
                last.then_inc(rlt_filled.sem, 1)

            def positions(t):
                b = ot_bank[:, POS_COLS]
                pe.wait_ge(m_ready.sem, t.value(m_ready))
                pe.wait_ge(pos_used.sem, t.value(pos_used, back=1))
                pe.wait_ge(ot_evac.sem, t.value(ot_evac))
                nc.tensor.matmul(b[:, 0:E], before[:, :], M[:, 0, :], start=True, stop=True)
                nc.tensor.matmul(b[:, E:2 * E], ones_b[:, :], M[:, 0, :], start=True, stop=False)
                nc.tensor.matmul(b[:, E:2 * E], before[:, :], M[:, 1, :], start=False, stop=True)
                nc.tensor.matmul(b[:, 2 * E:3 * E], ones_b[:, :], M[:, 0, :], start=True, stop=False)
                nc.tensor.matmul(b[:, 2 * E:3 * E], ones_b[:, :], M[:, 1, :], start=False, stop=True).then_inc(pos_filled.sem, 1)

            def gate_up(t, m):
                b = take(f"GU{m}", t, JOBS)
                for a in range(2):
                    for c in range(KC):
                        last = split_product(b[:, a * TB:(a + 1) * TB],
                                             both(wsgu, ALL, c, slice(a * F + m * P, a * F + (m + 1) * P)),
                                             both(XT, ALL, c, ALL), c == 0, c == KC - 1)
                last.then_inc(gu_filled.sem, 1)

            def down(t, tile, parts=range(FC)):
                b = take(f"DN{tile}", t, JOBS) if 0 in parts else bank_of(f"DN{tile}")
                for m in parts:
                    pe.wait_ge(hl_ready.sem, t.value(hl_ready, m))
                    last = split_product(b[:, :], both(HT, ALL, m, slice(tile * P, (tile + 1) * P)), both(wsd, ALL, m, ALL),
                                         m == 0, m == FC - 1)
                if FC - 1 in parts:
                    last.then_inc(dn_filled.sem, 1)

            pe.wait_ge(consts_made, 1)
            pe.wait_ge(consts_done, 1)
            pe.wait_ge(weights_in, 16 * WEIGHT_DMAS)
            for c in range(KC):
                last = nc.tensor.transpose(bank[0][:, c * E:(c + 1) * E], rw[:, c * P:(c + 1) * P], ident[0:E, 0:E])
            last.then_inc(rw_turned, 1)
            pe.wait_ge(rw_ready, 3)
            pe.wait_ge(w_low, len(staged) + 1)
            first = Turn(0, 0)
            for k in range(2):
                xt(first, k)
            gate1(first, PROJECT)
            project(first, 0, wq, q_filled, ("Qa", "Qb"), PROJECT)
            for k in range(2):
                gate2(first, k, PROJECT)
            project(first, 1, wq, q_filled, ("Qa", "Qb"), PROJECT)
            for k in range(2):
                project(first, k, wk, k_filled, ("Ka", "Kb"), PROJECT)
            for k in range(2):
                values(first, k, PROJECT)
            for k in range(2):
                ktok(first, k, PROJECT)
            pe.wait_ge(v_ready.sem, first.value(v_ready))
            pe.wait_ge(ktok_ready.sem, first.value(ktok_ready))
            for odd in range(2):
                state_updates(first, odd, PROJECT)
            for k in range(2):
                xt(first.next(), k)
            with pe.Fori(0, NBLK // 2) as pair:
                for odd in range(2):
                    t = Turn(pair, odd)
                    scores(t, 0, (0, 1))
                    gate1(t)
                    scores(t, 0, (2, 3))
                    project(t, 0, wq, q_filled, ("Qa", "Qb"))
                    scores(t, 1, (0, 1))
                    gate2(t, 0)
                    turn_probs(t, 0)
                    project(t, 0, wk, k_filled, ("Ka", "Kb"), parts=(0,))
                    scores(t, 1, (2, 3))
                    gate2(t, 1)
                    outputs(t, 0)
                    project(t, 0, wk, k_filled, ("Ka", "Kb"), parts=(1,))
                    scores(t, 2, (0, 1))
                    project(t, 1, wq, q_filled, ("Qa", "Qb"), parts=(0,))
                    turn_probs(t, 1)
                    scores(t, 2, (2, 3))
                    project(t, 1, wq, q_filled, ("Qa", "Qb"), parts=(1,))
                    outputs(t, 1)
                    project(t, 1, wk, k_filled, ("Ka", "Kb"), parts=(0,))
                    scores(t, 3, (0, 1))
                    values(t, 0, chunks=(0, 1))
                    turn_probs(t, 2)
                    scores(t, 3, (2, 3))
                    project(t, 1, wk, k_filled, ("Ka", "Kb"), parts=(1,))
                    turn_out(t, 0)
                    outputs(t, 2)
                    values(t, 0, chunks=(2, 3))
                    turn_probs(t, 3)
                    values(t, 1, chunks=(0,))
                    outputs(t, 3)
                    values(t, 1, chunks=(1,))
                    turn_out(t, 1)
                    values(t, 1, chunks=(2,))
                    x2t(t, 0)
                    values(t, 1, chunks=(3,))
                    x2t(t, 1)
                    router(t)
                    gate_up(t, 0)
                    turn_logits(t)
                    gate_up(t, 1)
                    gate_up(t, 2)
                    ktok(t, 0)
                    xt(t.next(2), 0)
                    ktok(t, 1)
                    xt(t.next(2), 1)
                    down(t, 0, (0, 1))
                    state_updates(t, 0)
                    down(t, 0, (2,))
                    down(t, 1, (0,))
                    state_updates(t, 1)
                    down(t, 1, (1, 2))
                    positions(t)

        @block.vector
        def _(dve):
            LINKS = 51
            links = [0, None]

            def link(ins):
                ins.then_inc(dve_chain, 1)
                links[0] += 1
                t = links[1]
                dve.wait_ge(dve_chain, links[0] if t is None else t.pair * (2 * LINKS) + (START + t.odd * LINKS + links[0]))

            v = nc.vector

            def bc(ap, n):
                return ap.unsqueeze(2).to_broadcast([ap.shape[0], ap.shape[1], n])

            def mid(ap, n):
                return ap.unsqueeze(1).to_broadcast([ap.shape[0], n, ap.shape[1]])

            def segs(ap):
                return ap.rearrange("p c (s t) -> p (c s) t", t=HC)

            def norm1(t):
                dve.wait_ge(x_loaded.sem, t.value(x_loaded))
                for k in range(NT):
                    ins = v.bn_stats(st1[:, k, :], X[t.buf][:, k, :])
                link(ins)
                apart(dve, dve_apart)
                for k in range(NT):
                    ins = v.bn_aggr(mv1[:, k, :], st1[:, k, :])
                link(ins)
                v.tensor_scalar(ve1[:, :], mv1[:, :, 1], EPS, None, ALU.add).then_inc(var1_ready.sem, 1)

            def shift1(t):
                dve.wait_ge(rstd1_ready.sem, t.value(rstd1_ready))
                dve.wait_ge(xn_ready.sem, t.value(xn_ready, back=1))
                v.scalar_tensor_tensor(sh1[:, :], mv1[:, :, 0], -1.0, rs1[:, :], ALU.mult, ALU.mult).then_inc(shift1_ready.sem, 1)

            def silu1(t):
                dve.wait_ge(g1_tanh.sem, t.value(g1_tanh))
                dve.wait_ge(g2_filled.sem, t.value(g2_filled, back=1))
                v.scalar_tensor_tensor(s1[:, :], t1[:, :], 1.0, z1[:, :], ALU.add, ALU.mult).then_inc(s1_ready.sem, 1)

            def decays(t):
                dve.wait_ge(al_ready.sem, t.value(al_ready))
                dve.wait_ge(qd_ready.sem, t.value(qd_ready, back=1))
                v.memset(segs(EX[:, :, :])[:, :, 0:1], 0.0)
                link(v.tensor_copy(segs(EX[:, :, :])[:, :, 1:HC], segs(AL[:, :, :])[:, :, 0:HC - 1]))
                for m in range(KC):
                    ins = v.tensor_tensor_scan(EX[:, m, :], EX[:, m, :], seg_start[:, :], 0.0, ALU.mult, ALU.add)
                link(ins)
                link(v.tensor_tensor(AL[:, :, :], EX[:, :, :], AL[:, :, :], ALU.mult))

            def products(t):
                v.tensor_copy(FS[t.buf][:, :, :, :].rearrange("p c n a -> p (c n a)"),
                              segs(AL[:, :, :])[:, :, HC - 1]).then_inc(fs_ready.sem, 1)
                dve.wait_ge(fs_ready.sem, t.value(fs_ready))

            def inverse(t, m):
                ins = v.reciprocal(AL[:, m, :], AL[:, m, :])
                if m == KC - 1:
                    ins.then_inc(inverted.sem, 1)
                else:
                    link(ins)

            def values(t, k):
                dve.wait_ge(v_filled.sem, t.value(v_filled, k))
                if k == 0:
                    dve.wait_ge(ot_filled.sem, t.value(ot_filled, back=1))
                    dve.wait_ge(dk_filled.sem, t.value(dk_filled, back=1))
                    dve.wait_ge(v_swapped.sem, t.value(v_swapped, back=1))
                v.tensor_tensor(V[:, k, :], bank_of(f"V{k}")[:, :], bvb[:, :], ALU.add).then_inc(v_ready.sem, 1)

            def state(t, chunks):
                dve.wait_ge(dk_filled.sem, t.value(dk_filled))
                dve.wait_ge(ot_filled.sem, t.value(ot_filled, back=1))
                for c in chunks:
                    mid_f, end_f = FS[t.buf][:, :, c, 0], FS[t.buf][:, :, c, 1]
                    if c == 0:
                        ins = v.scalar_tensor_tensor(R[:, c, :, :], S[:, :, :], keep[:, bass.ds(t.pair * 2 + t.odd, 1)],
                                                     bc(mid_f, D), ALU.mult, ALU.mult)
                    else:
                        ins = v.tensor_tensor(R[:, c, :, :], S[:, :, :], bc(mid_f, D), ALU.mult)
                    ins.then_inc(r_ready.sem, 1)
                    dve.wait_ge(r_ready.sem, t.value(r_ready, c))
                    dk = bank_of("DK")[:, c * P:(c + 1) * P].rearrange("p (g e) -> p g e", g=KC)
                    ins = v.tensor_tensor(U[:, :, :], R[:, c, :, :], dk, ALU.add)
                    if c == NCH - 1:
                        ins.then_inc(dk_used.sem, 1)
                        dve.wait_ge(dk_used.sem, t.value(dk_used))
                    else:
                        link(ins)
                    link(v.tensor_tensor(S[:, :, :], U[:, :, :], bc(end_f, D), ALU.mult))

            def softmax_a(t, u):
                dve.wait_ge(s_filled.sem, t.value(s_filled, u))
                pr = PR[u % 2][:, :, :]
                if u >= 2:
                    dve.wait_ge(pt_filled.sem, t.value(pt_filled, u - 2))
                else:
                    dve.wait_ge(pt_filled.sem, t.value(pt_filled, back=1))
                v.tensor_tensor(pr, s_bank[:, :].rearrange("p (n k) -> p n k", k=C), mid(causal[:, :], 8),
                                ALU.add).then_inc(s_masked.sem, 1)
                dve.wait_ge(s_masked.sem, t.value(s_masked, u))
                link(v.tensor_reduce(MX[:, :], pr, AX.X, ALU.max))
                v.tensor_tensor(pr, pr, bc(MX[:, :], C), ALU.subtract).then_inc(shifted.sem, 1)
                dve.wait_ge(a_filled.sem, t.value(a_filled, u))
                v.tensor_tensor(AM[u % 2][:, :, :], a_bank[:, :].rearrange("p (n k) -> p n k", k=P),
                                mid(decay_mask[:, :], 4), ALU.mult).then_inc(a_masked.sem, 1)

            def softmax_b(t, u):
                dve.wait_ge(exped.sem, t.value(exped, u))
                link(v.tensor_reduce(SU[:, :], PR[u % 2][:, :, :], AX.X, ALU.add))
                link(v.reciprocal(RU[:, :], SU[:, :]))
                v.tensor_tensor(PR[u % 2][:, :, :], PR[u % 2][:, :, :], bc(RU[:, :], C), ALU.mult).then_inc(p_ready.sem, 1)

            def weights(t, u):
                dve.wait_ge(pt_filled.sem, t.value(pt_filled, u))
                dve.wait_ge(a_masked.sem, t.value(a_masked, u))
                if u >= 2:
                    dve.wait_ge(ot_filled.sem, t.value(ot_filled, u - 2))
                else:
                    dve.wait_ge(ot_filled.sem, t.value(ot_filled, back=1))
                v.tensor_tensor(WT[u % 2][:, :, :], pt_bank[:, :].rearrange("p (n k) -> p n k", k=P), AM[u % 2][:, :, :],
                                ALU.add).then_inc(w_ready.sem, 1)

            def residual(t, k):
                dve.wait_ge(at_filled.sem, t.value(at_filled, k))
                if k == 0:
                    dve.wait_ge(out_stored.sem, t.value(out_stored, back=1))
                v.tensor_tensor(X2[:, k, :], bank_of(f"ATr{k}")[:, :], X[t.buf][:, k, :], ALU.add).then_inc(x2_ready.sem, 1)
                dve.wait_ge(x2_ready.sem, t.value(x2_ready, k))
                link(v.bn_stats(st2[:, k, :], X2[:, k, :]))
                apart(dve, dve_apart)
                link(v.bn_aggr(mv2[:, k, :], st2[:, k, :]))
                v.tensor_scalar(ve2[:, k:k + 1], mv2[:, k, 1:2], EPS, None, ALU.add).then_inc(var2_ready.sem, 1)

            def norm2(t, k):
                dve.wait_ge(rstd2_ready.sem, t.value(rstd2_ready, k))
                if k == 0:
                    dve.wait_ge(rows_stored.sem, t.value(rows_stored, back=1))
                    dve.wait_ge(x2t_filled.sem, t.value(x2t_filled, back=1))
                v.tensor_scalar(XR[:, k, 0:DIM], X2[:, k, :], mv2[:, k, 0:1], rs2[:, k:k + 1],
                                ALU.subtract, ALU.mult).then_inc(x2n_ready.sem, 1)

            def route_a(t):
                dve.wait_ge(rlt_filled.sem, t.value(rlt_filled))
                lg = bank_of("RLT")[:, 0:NT * E].rearrange("p (a b) -> p a b", a=NT)
                link(v.tensor_reduce(rmx[:, :], lg, AX.X, ALU.max))
                v.tensor_tensor(LG[:, :, :], lg, bc(rmx[:, :], E), ALU.subtract).then_inc(logits_shifted.sem, 1)

            def route_b(t):
                dve.wait_ge(router_exped.sem, t.value(router_exped))
                link(v.tensor_reduce(rsu[:, :], PB[:, :, :], AX.X, ALU.add))
                link(v.reciprocal(rre[:, :], rsu[:, :]))
                link(v.tensor_tensor(PB[:, :, :], PB[:, :, :], bc(rre[:, :], E), ALU.mult))
                apart(dve, dve_apart)
                for k in range(NT):
                    ins = v.max(top[:, k, :], PB[:, k, :])
                link(ins)
                apart(dve, dve_apart)
                for k in range(NT):
                    ins = v.match_replace(RP[:, k, :], top[:, k, :], PB[:, k, :], -1.0)
                link(ins)
                dve.wait_ge(pos_filled.sem, t.value(pos_filled, back=1))
                v.tensor_tensor(M[:, :, :], RP[:, :, :], PB[:, :, :], ALU.is_lt).then_inc(m_ready.sem, 1)
                dve.wait_ge(m_ready.sem, t.value(m_ready))
                link(v.tensor_tensor(PW[:, :, :], PB[:, :, :], M[:, :, :], ALU.mult))
                link(v.tensor_reduce(rsu[:, :], PW[:, :, :], AX.X, ALU.add))
                link(v.reciprocal(rre[:, :], rsu[:, :]))
                v.tensor_tensor(XR[:, :, DIM:ROW], PW[:, :, :], bc(rre[:, :], E), ALU.mult).then_inc(rows_ready.sem, 1)

            def route_c(t):
                dve.wait_ge(pos_filled.sem, t.value(pos_filled))
                b = ot_bank[:, POS_COLS]
                link(v.tensor_tensor(PO[:, :, :], b[:, 0:NT * E].rearrange("p (a b) -> p a b", a=NT), mid(carry[:, :], NT), ALU.add))
                v.tensor_tensor(carry[:, :], carry[:, :], b[:, NT * E:(NT + 1) * E], ALU.add).then_inc(pos_used.sem, 1)
                v.scalar_tensor_tensor(VA[:, :, :], PO[:, :, :], float(CAP), M[:, :, :], ALU.is_lt, ALU.mult)
                link(v.tensor_scalar(T1[:, :, :], PO[:, :, :], float(P), float(P * P - 1), ALU.is_ge, ALU.mult))
                link(v.scalar_tensor_tensor(T2[:, :, :], PO[:, :, :], float(P), T1[:, :, :], ALU.mult, ALU.subtract))
                link(v.tensor_tensor(T1[:, :, :], T2[:, :, :], mid(slot_base[:, :], NT), ALU.add))
                link(v.tensor_scalar(T2[:, :, :], T1[:, :, :], -1.0, float(NOWHERE), ALU.mult, ALU.add))
                link(v.tensor_tensor(T1[:, :, :], T2[:, :, :], VA[:, :, :], ALU.mult))
                apart(dve, dve_apart)
                for k in range(NT):
                    ins = v.max(key8[:, k, :], T1[:, k, :])
                link(ins)
                dve.wait_ge(slots_used.sem, t.value(slots_used, back=1))
                v.tensor_copy(toki[:, :], tokf[:, :])
                v.tensor_scalar(slot8[:, :, :], key8[:, :, :], -1.0, float(NOWHERE), ALU.mult, ALU.add).then_inc(slots_ready.sem, 1)
                dve.wait_ge(slots_ready.sem, t.value(slots_ready))
                link(v.tensor_scalar(tokf[:, :], tokf[:, :], float(TB), None, ALU.add))

            def low_part(filled, ready, t, k, source):
                dve.wait_ge(filled.sem, t.value(filled, k))
                half = slice(2 * k, 2 * k + 2)
                v.tensor_tensor(XT[1][:, half, :], source[:, :].rearrange("p (a b) -> p a b", a=2),
                                XT[0][:, half, :].bitcast(f32), ALU.subtract).then_inc(ready.sem, 1)

            def xt_low(t):
                for k in range(2):
                    low_part(xh_ready, xl_ready, t, k, XT_BANK[k])

            def x2t_low(t):
                for k in range(2):
                    low_part(x2h_ready, x2l_ready, t, k, bank_of("X2Ta" if k == 0 else "X2Tb"))

            def hidden(t, m):
                dve.wait_ge(gu_tanh.sem, t.value(gu_tanh, m))
                dve.wait_ge(hl_ready.sem, t.value(hl_ready, m - 1) if m else t.value(hl_ready, back=1))
                b = bank_of(f"GU{m}")
                link(v.scalar_tensor_tensor(WG[:, :], TG[:, :], 1.0, b[:, 0:TB], ALU.add, ALU.mult))
                v.scalar_tensor_tensor(WG[:, :], WG[:, :], 0.5, b[:, TB:2 * TB], ALU.mult, ALU.mult).then_inc(gu_ready.sem, 1)

            def hidden_low(t, m):
                dve.wait_ge(hh_ready.sem, t.value(hh_ready, m))
                dve.wait_ge(gu_ready.sem, t.value(gu_ready, m))
                if m == 0:
                    dve.wait_ge(dn_filled.sem, t.value(dn_filled, back=1))
                v.tensor_tensor(HT[1][:, m, :], WG[:, :], HT[0][:, m, :].bitcast(f32), ALU.subtract).then_inc(hl_ready.sem, 1)

            def total(t, k):
                dve.wait_ge(dn_filled.sem, t.value(dn_filled, k))
                v.tensor_tensor(X2[:, k, :], bank_of(f"DN{k}")[:, :], X2[:, k, :], ALU.add).then_inc(out_ready.sem, 1)

            v.memset(a_bank[:, :], 0.0)
            v.memset(carry[:, :], 0.0)
            v.memset(S[:, :, :], 0.0).then_inc(consts_done, 1)
            dve.wait_ge(consts_done, 1)
            dve.wait_ge(consts_made, 1)
            for i, (piece, high, low, _) in enumerate(staged):
                if i < len(piece_in):
                    dve.wait_ge(piece_in[i], 16)
                dve.wait_ge(w_high, i + 1)
                v.tensor_tensor(low, piece, high.bitcast(f32), ALU.subtract).then_inc(w_low, 1)
            dve.wait_ge(weights_in, 16 * WEIGHT_DMAS)
            dve.wait_ge(rw_ready, 1)
            v.tensor_tensor(rwT[1][:, :, :], bank[0][:, 0:KC * E].rearrange("p (a b) -> p a b", a=KC),
                            rwT[0][:, :, :].bitcast(f32), ALU.subtract).then_inc(w_low, 1)
            dve.wait_ge(w_low, len(staged) + 1)
            t = Turn(0, 0)
            norm1(t)
            shift1(t)
            xt_low(t)
            silu1(t)
            decays(t)
            products(t)
            for m in range(KC):
                inverse(t, m)
            for k in range(NT):
                values(t, k)
            norm1(t.next())
            shift1(t.next())
            xt_low(t.next())
            START = links[0]
            with dve.Fori(0, NBLK // 2) as pair:
                for odd in range(2):
                    t = Turn(pair, odd)
                    n = t.next()
                    links[0], links[1] = 0, t
                    softmax_a(t, 0)
                    silu1(n)
                    softmax_b(t, 0)
                    state(t, (0, 1))
                    weights(t, 0)
                    softmax_a(t, 1)
                    state(t, (2, 3))
                    softmax_b(t, 1)
                    decays(n)
                    products(n)
                    weights(t, 1)
                    softmax_a(t, 2)
                    softmax_b(t, 2)
                    inverse(n, 0)
                    weights(t, 2)
                    softmax_a(t, 3)
                    residual(t, 0)
                    softmax_b(t, 3)
                    norm2(t, 0)
                    weights(t, 3)
                    inverse(n, 1)
                    values(n, 0)
                    residual(t, 1)
                    norm2(t, 1)
                    values(n, 1)
                    x2t_low(t)
                    inverse(n, 2)
                    norm1(t.next(2))
                    inverse(n, 3)
                    hidden(t, 0)
                    route_a(t)
                    hidden_low(t, 0)
                    shift1(t.next(2))
                    hidden(t, 1)
                    hidden_low(t, 1)
                    hidden(t, 2)
                    hidden_low(t, 2)
                    xt_low(t.next(2))
                    route_b(t)
                    total(t, 0)
                    total(t, 1)
                    route_c(t)
                    assert links[0] == LINKS, links[0]


def phase_experts(nc, w_gate, w_up, w_down, out_flat, norm_dram, table_dram):
    ctx = ExitStack()
    with ctx:
        def sb(name, shape, dt=f32):
            return ctx.enter_context(nc.sbuf_tensor(name, shape, dt))

        def sem(name):
            return ctx.enter_context(nc.semaphore(name))

        ident = sb("ident2", [P, P])
        tokens = sb("tokens", [P, ST * (E + 2)], i32)
        WS = [sb(f"WS{i}", [P, WCOLS]) for i in range(2)]
        WH = [sb(f"WH{i}", [P, WCOLS], f32r) for i in range(2)]
        WL = [sb(f"WL{i}", [P, WCOLS], f32r) for i in range(2)]
        XG = [sb(f"XG{i}", [P, ST, ROW + 1]) for i in range(2)]
        XH = [sb(f"XH{i}", [P, KC, CAP], f32r) for i in range(2)]
        XL = [sb(f"XL{i}", [P, KC, CAP], f32r) for i in range(2)]
        row_at = [sb(f"row_at{i}", [P, ST], i32) for i in range(2)]
        sum_at = sb("sum_at", [P, ST], i32)
        WC = [sb(f"WC{i}", [P, ST]) for i in range(2)]
        OG = sb("OG", [P, ST, DIM])
        TG = sb("TGe", [P, CAP])
        WG = sb("WGe", [P, CAP])
        HF = sb("HF", [P, FC, CAP])
        HH = sb("HH", [P, FC, CAP], f32r)
        HL = sb("HL", [P, FC, CAP], f32r)
        bank = [ctx.enter_context(nc.psum_tensor(f"ebank{i}", [P, 512], f32)) for i in range(7)]
        TURN, HID, DOWN = (0, 1), (2, 3, 4), (5, 6)

        primed = []

        def event(name, n=1):
            primed.append(Event(sem(name), n, n))
            return primed[-1]

        ident_made = sem("ident_made")
        table_in = sem("table_in")
        pool_apart = sem("pool_apart2")
        cleared = sem("cleared")
        begun = sem("begun2")
        w_in = [sem(f"expert_weights_in{i}") for i in range(2)]
        row_at_ready = event("row_at_ready")
        sum_at_ready = event("sum_at_ready")
        wc_ready = event("wc_ready")
        gathered = [sem(f"rows_gathered{i}") for i in range(2)]
        sums_in = Event(sem("sums_gathered"), 16 * ST, 0)
        sums_out = Event(sem("sums_scattered"), 16 * ST, 0)
        xe_filled = event("xe_filled", 2)
        xh_ready = event("xh_ready", 2)
        xl_ready = event("xl_ready", 2)
        wh_ready = event("wh_ready", len(PIECES))
        wl_ready = event("wl_ready", len(PIECES))
        gu_filled = event("e_gu_filled", 3)
        gu_tanh = event("e_gu_tanh", 3)
        hf_ready = event("hf_ready", 3)
        hh_ready = event("hh_ready", 3)
        hl_ready = event("hl_ready", 3)
        dn_filled = event("e_dn_filled", 2)
        sum_ready = event("sum_ready", 2)

        block = ctx.enter_context(nc.Block())

        @block.sync
        def _(sp):
            sp.wait_ge(begun, 1)
            sp.dma_start(tokens[:, 0:ST * E], table_dram.rearrange("(p c) o -> p (c o)", p=P)).then_inc(table_in, 16)

            def load(t, e, split=None):
                for i, (src, chunks) in enumerate(((w_gate, KC), (w_up, KC), (w_down, FC))):
                    if split:
                        sp.wait_ge(wl_ready.sem, split.value(wl_ready, (1, 3, 6)[i]))
                    sp.dma_start(WS[t.buf][:, i * WPART:(i + 1) * WPART].rearrange("p (c n) -> p c n", c=chunks),
                                 src.rearrange("e (c p) n -> e p c n", p=P)[e, :, :, :]).then_inc(w_in[t.buf], 16)

            for odd in range(2):
                load(Turn(0, odd), odd)
            with sp.Fori(0, E // 2 - 1) as pair:
                for odd in range(2):
                    t = Turn(pair, odd)
                    load(t, pair * 2 + (odd + 2), split=t)
            t = Turn(E // 2 - 1, 0)
            load(t, 0, split=t)
            sp.wait_ge(w_in[0], 48 * (E // 2 + 1))
            sp.wait_ge(w_in[1], 48 * (E // 2))

        @block.gpsimd
        def _(pool):
            for ev in primed:
                pool.sem_inc(ev.sem, ev.early)
            pool.sem_inc(begun, 1)
            nc.gpsimd.memset(ident[:, :], 0.0).then_inc(ident_made, 1)
            pool.wait_ge(ident_made, 1)
            nc.gpsimd.affine_select(out=ident[:, :], in_=ident[:, :], compare_op=ALU.not_equal, fill=1.0,
                                    base=0, pattern=[[-1, P]], channel_multiplier=1).then_inc(ident_made, 1)
            pool.wait_ge(table_in, 16)
            pool.wait_ge(cleared, 1)

            def gather_rows(t):
                nc.gpsimd.tensor_copy(row_at[t.buf][:, :], tokens[:, bass.ds(t.pair * (2 * ST) + t.odd * ST, ST)]).then_inc(row_at_ready.sem, 1)
                pool.wait_ge(row_at_ready.sem, t.value(row_at_ready))
                apart(pool, pool_apart)
                for k in range(ST):
                    nc.gpsimd.indirect_dma_start(
                        out=XG[t.buf][:, k, 0:ROW], out_offset=None, in_=norm_dram,
                        in_offset=bass.IndirectOffsetOnAxis(ap=row_at[t.buf][:, k:k + 1], axis=0), bounds_check=NTOK - 1,
                        oob_is_err=False).then_inc(gathered[t.buf], 16)

            def gather_sums(t):
                nc.gpsimd.tensor_copy(sum_at[:, :], tokens[:, bass.ds(t.pair * (2 * ST) + t.odd * ST, ST)]).then_inc(sum_at_ready.sem, 1)
                pool.wait_ge(sum_at_ready.sem, t.value(sum_at_ready))
                apart(pool, pool_apart)
                for k in range(ST):
                    nc.gpsimd.indirect_dma_start(
                        out=OG[:, k, :], out_offset=None, in_=out_flat,
                        in_offset=bass.IndirectOffsetOnAxis(ap=sum_at[:, k:k + 1], axis=0), bounds_check=NTOK - 1,
                        oob_is_err=False).then_inc(sums_in.sem, 16)

            def store_sums(t):
                for k in range(ST):
                    pool.wait_ge(sum_ready.sem, t.value(sum_ready, k))
                    apart(pool, pool_apart)
                    nc.gpsimd.indirect_dma_start(
                        out=out_flat, out_offset=bass.IndirectOffsetOnAxis(ap=sum_at[:, k:k + 1], axis=0),
                        in_=OG[:, k, :], in_offset=None, bounds_check=NTOK - 1,
                        oob_is_err=False).then_inc(sums_out.sem, 16)
                pool.wait_ge(sums_out.sem, t.value(sums_out))
                apart(pool, pool_apart)

            gather_rows(Turn(0, 0))
            gather_sums(Turn(0, 0))
            gather_rows(Turn(0, 1))
            with pool.Fori(0, E // 2) as pair:
                for odd in range(2):
                    t = Turn(pair, odd)
                    pool.wait_ge(xe_filled.sem, t.value(xe_filled))
                    pool.wait_ge(wc_ready.sem, t.value(wc_ready))
                    pool.wait_ge(gathered[t.buf], t.pair * (16 * ST) + 16 * ST)
                    gather_rows(Turn(pair, odd + 2))
                    store_sums(t)
                    gather_sums(t.next())
            pool.wait_ge(gathered[0], 16 * ST * (E // 2 + 1))
            pool.wait_ge(gathered[1], 16 * ST * (E // 2 + 1))
            pool.wait_ge(sums_in.sem, 16 * ST * (E + 1))

        @block.scalar
        def _(act):
            def xh(t):
                for k in range(ST):
                    act.wait_ge(xe_filled.sem, t.value(xe_filled, k))
                    nc.scalar.activation(XH[t.buf][:, :, k * P:(k + 1) * P], bank[TURN[k]][:, :].rearrange("p (c s) -> p c s", c=KC),
                                         ACT.Copy).then_inc(xh_ready.sem, 1)

            def split_high(t, i):
                if i == 0:
                    act.wait_ge(w_in[t.buf], t.pair * 48 + 48 * (t.odd // 2 + 1))
                cols = PIECES[i]
                nc.scalar.activation(WH[t.buf][:, cols], WS[t.buf][:, cols], ACT.Copy).then_inc(wh_ready.sem, 1)

            def hidden_high(t, m):
                act.wait_ge(hf_ready.sem, t.value(hf_ready, m))
                nc.scalar.activation(HH[:, m, :], HF[:, m, :], ACT.Copy).then_inc(hh_ready.sem, 1)

            for i in range(len(PIECES)):
                split_high(Turn(0, 0), i)
            xh(Turn(0, 0))
            with act.Fori(0, E // 2) as pair:
                for odd in range(2):
                    t = Turn(pair, odd)
                    act.wait_ge(dn_filled.sem, t.value(dn_filled, back=1))
                    for m in range(FC):
                        act.wait_ge(gu_filled.sem, t.value(gu_filled, m))
                        act.wait_ge(hf_ready.sem, t.value(hf_ready, m - 1) if m else t.value(hf_ready, back=1))
                        nc.scalar.activation(TG[:, :], bank[HID[m]][:, 0:CAP], ACT.Tanh, scale=0.5).then_inc(gu_tanh.sem, 1)
                        if m < 2:
                            split_high(t.next(), 2 * m)
                        hidden_high(t, m)
                        if m < 2:
                            split_high(t.next(), 2 * m + 1)
                    xh(t.next())
                    for i in range(4, len(PIECES)):
                        split_high(t.next(), i)

        @block.tensor
        def _(pe):
            pe.wait_ge(ident_made, 2)

            def turn_rows(t):
                for k in range(ST):
                    pe.wait_ge(gathered[t.buf], t.pair * (16 * ST) + 16 * ST * (t.odd // 2 + 1))
                    pe.wait_ge(xl_ready.sem, t.value(xl_ready, k, back=1))
                    for c in range(KC):
                        last = nc.tensor.transpose(bank[TURN[k]][:, c * P:(c + 1) * P], XG[t.buf][:, k, c * P:(c + 1) * P], ident[:, :])
                    last.then_inc(xe_filled.sem, 1)

            turn_rows(Turn(0, 0))
            with pe.Fori(0, E // 2) as pair:
                for odd in range(2):
                    t = Turn(pair, odd)
                    pe.wait_ge(wl_ready.sem, t.value(wl_ready, 3))
                    pe.wait_ge(xl_ready.sem, t.value(xl_ready))
                    for m in range(FC):
                        pe.wait_ge(hf_ready.sem, t.value(hf_ready, m, back=1))
                        for a in range(2):
                            for c in range(KC):
                                at = a * WPART + c * F + m * P
                                high, low = WH[odd][:, at:at + P], WL[odd][:, at:at + P]
                                for i, (w, x) in enumerate(((high, XH), (high, XL), (low, XH))):
                                    last = nc.tensor.matmul(bank[HID[m]][:, a * CAP:(a + 1) * CAP], w, x[odd][:, c, :],
                                                            start=(c == 0 and i == 0), stop=(c == KC - 1 and i == 2))
                        last.then_inc(gu_filled.sem, 1)
                    turn_rows(t.next())
                    pe.wait_ge(wl_ready.sem, t.value(wl_ready))
                    for m, k in ((0, 0), (1, 0), (0, 1), (1, 1), (2, 0), (2, 1)):
                        if m == 0:
                            pe.wait_ge(sum_ready.sem, t.value(sum_ready, k, back=1))
                        if k == 0:
                            pe.wait_ge(hl_ready.sem, t.value(hl_ready, m))
                        at = 2 * WPART + m * DIM
                        high, low = HH[:, m, k * P:(k + 1) * P], HL[:, m, k * P:(k + 1) * P]
                        for i, (h, w) in enumerate(((high, WH), (high, WL), (low, WH))):
                            last = nc.tensor.matmul(bank[DOWN[k]][:, :], h, w[odd][:, at:at + DIM],
                                                    start=(m == 0 and i == 0), stop=(m == FC - 1 and i == 2))
                        if m == FC - 1:
                            last.then_inc(dn_filled.sem, 1)

        @block.vector
        def _(dve):
            v = nc.vector
            wg_ready = sem("wg_ready")
            v.memset(tokens[:, ST * E:], NOWHERE)
            v.memset(OG[:, :, :], 0.0)
            v.memset(XG[1][:, :, :], 0.0)
            v.memset(XG[0][:, :, :], 0.0).then_inc(cleared, 1)
            def take_weights(t):
                dve.wait_ge(gathered[t.buf], t.pair * (16 * ST) + 16 * ST * (t.odd // 2 + 1))
                v.tensor_copy(WC[t.buf][:, :], XG[t.buf][:, :, bass.ds(t.pair * 2 + (DIM + t.odd), 1)]
                              .rearrange("p k o -> p (k o)")).then_inc(wc_ready.sem, 1)
                dve.wait_ge(wc_ready.sem, t.value(wc_ready))

            def split_low(t, i):
                dve.wait_ge(wh_ready.sem, t.value(wh_ready, i))
                cols = PIECES[i]
                v.tensor_tensor(WL[t.buf][:, cols], WS[t.buf][:, cols], WH[t.buf][:, cols].bitcast(f32),
                                ALU.subtract).then_inc(wl_ready.sem, 1)

            def xl(t):
                for k in range(ST):
                    dve.wait_ge(xh_ready.sem, t.value(xh_ready, k))
                    part = slice(k * P, (k + 1) * P)
                    v.tensor_tensor(XL[t.buf][:, :, part], bank[TURN[k]][:, :].rearrange("p (c s) -> p c s", c=KC),
                                    XH[t.buf][:, :, part].bitcast(f32), ALU.subtract).then_inc(xl_ready.sem, 1)

            def hidden_low(t, m):
                dve.wait_ge(hh_ready.sem, t.value(hh_ready, m))
                if m == 0:
                    dve.wait_ge(dn_filled.sem, t.value(dn_filled, back=1))
                v.tensor_tensor(HL[:, m, :], HF[:, m, :], HH[:, m, :].bitcast(f32), ALU.subtract).then_inc(hl_ready.sem, 1)

            for i in range(len(PIECES)):
                split_low(Turn(0, 0), i)
            xl(Turn(0, 0))
            take_weights(Turn(0, 0))
            with dve.Fori(0, E // 2) as pair:
                for odd in range(2):
                    t = Turn(pair, odd)
                    for m in range(FC):
                        dve.wait_ge(gu_tanh.sem, t.value(gu_tanh, m))
                        b = bank[HID[m]]
                        v.scalar_tensor_tensor(WG[:, :], TG[:, :], 1.0, b[:, 0:CAP], ALU.add, ALU.mult).then_inc(wg_ready, 1)
                        dve.wait_ge(wg_ready, pair * 6 + (3 * odd + m + 1))
                        dve.wait_ge(hl_ready.sem, t.value(hl_ready, m, back=1))
                        v.scalar_tensor_tensor(HF[:, m, :], WG[:, :], 0.5, b[:, CAP:2 * CAP], ALU.mult,
                                               ALU.mult).then_inc(hf_ready.sem, 1)
                        dve.wait_ge(hf_ready.sem, t.value(hf_ready, m))
                        if m < 2:
                            split_low(t.next(), 2 * m)
                        hidden_low(t, m)
                        if m < 2:
                            split_low(t.next(), 2 * m + 1)
                    xl(t.next())
                    for i in range(4, len(PIECES)):
                        split_low(t.next(), i)
                    take_weights(t.next())
                    dve.wait_ge(sums_in.sem, t.value(sums_in))
                    for k in range(ST):
                        dve.wait_ge(dn_filled.sem, t.value(dn_filled, k))
                        v.scalar_tensor_tensor(OG[:, k, :], bank[DOWN[k]][:, :], WC[odd][:, k:k + 1], OG[:, k, :], ALU.mult,
                                               ALU.add).then_inc(sum_ready.sem, 1)


_INS = ['L0_attn_x', 'L0_attn_Wq', 'L0_attn_bq', 'L0_attn_Wk', 'L0_attn_bk', 'L0_attn_Wv', 'L0_attn_bv',
        'L0_attn_Wg1', 'L0_attn_bg1', 'L0_attn_Wg2', 'L0_attn_bg2', 'L0_ffn_router_w', 'L0_ffn_w_gate',
        'L0_ffn_w_up', 'L0_ffn_w_down', 'L0_ffn_ws_gate_up', 'L0_ffn_ws_down']


def kernel(**inputs):
    import numpy as _np
    import concourse.bacc as _bacc
    from concourse import mybir as _mybir
    from concourse.bass_utils import run_bass_kernel_spmd as _run

    nc = _bacc.Bacc("TRN2", target_bir_lowering=False, num_devices=1)
    arrays, args = {}, []
    for name in _INS:
        a = _np.ascontiguousarray(inputs[name])
        arrays[f"in_{name}_dram"] = a
        args.append(nc.dram_tensor(f"in_{name}_dram", a.shape, _mybir.dt.from_np(a.dtype), kind="ExternalInput").ap())
    out = nc.dram_tensor("out_0_dram", (BATCH, LEN, DIM), _mybir.dt.float32, kind="ExternalOutput").ap()
    layer_kernel(nc, *args, out)
    r = _run(nc, [arrays], core_ids=[0])
    return r.results[0]["out_0_dram"]
```
